# Optimizing a Trainium2 kernel written in Bass

```python
import numpy as np
import jax
import jax.numpy as jnp

def _softmax(x, axis=-1):
    return jax.nn.softmax(x, axis=axis)

def _gelu(x):
    return jax.nn.gelu(x, approximate=True)

def _silu(x):
    return jax.nn.silu(x)

def _sigmoid(x):
    return jax.nn.sigmoid(x)

def _layernorm(x, axis=-1, eps=1e-05):
    m = jnp.mean(x, axis=axis, keepdims=True)
    v = jnp.var(x, axis=axis, keepdims=True)
    return (x - m) / jnp.sqrt(v + eps)

def _scatter_add(tgt, idx, src, axis=0):
    return tgt.at[idx].add(src)

def _segment_sum(src, seg, n):
    return jax.ops.segment_sum(src, seg, n)
kernel_name = 'mk_gnn_preln_d4_gnn_r8_8ecdad'

def setup_inputs(seed: int=0):
    np.random.seed(seed)
    _w = jnp.asarray

    def _rec_inputs():
        import jax
        import jax.numpy as jnp
        _gk = jax.random.key(seed)
        x = -0.0005121 + 1.001 * jax.random.normal(jax.random.fold_in(_gk, 1), (6250, 64), jnp.float32)
        src = jax.random.randint(jax.random.fold_in(_gk, 2), (200000,), 0, 6250, jnp.int32)
        dst = jax.random.randint(jax.random.fold_in(_gk, 3), (200000,), 0, 6250, jnp.int32)
        _o = jnp.argsort(dst, stable=True)
        src = src[_o]
        dst = dst[_o]
        edge_attr_32 = 0.000216709 + 1.00012 * jax.random.normal(jax.random.fold_in(_gk, 12), (200000, 32), jnp.float32)
        edge_attr_64 = -5.16925e-05 + 1.00005 * jax.random.normal(jax.random.fold_in(_gk, 13), (200000, 64), jnp.float32)
        return (x, src, dst, edge_attr_32, edge_attr_64)
    x, src, dst, edge_attr_32, edge_attr_64 = _rec_inputs()

    def _L0_gnn_setup():
        import jax, jax.numpy as jnp
        import numpy as np
        N_NODES = 6250
        N_EDGES = 100000
        D_NODE = 64
        D_EDGE = 32
        D_HID = 128

        def _mlp(x, W1, b1, W2, b2):
            return jax.nn.relu(x @ W1 + b1) @ W2 + b2
        key = jax.random.key(seed)
        ks = jax.random.split(key, 12)
        inp = {'nodes': jax.random.normal(ks[0], (N_NODES, D_NODE), dtype=jnp.float32), 'row': jax.random.randint(ks[1], (N_EDGES,), 0, N_NODES, dtype=jnp.int32), 'col': jax.random.randint(ks[2], (N_EDGES,), 0, N_NODES, dtype=jnp.int32), 'edge_features': jax.random.normal(ks[3], (N_EDGES, D_EDGE), dtype=jnp.float32)}
        d_in_msg = 2 * D_NODE + D_EDGE
        inp['mW1'] = jax.random.normal(ks[4], (d_in_msg, D_HID), dtype=jnp.float32) / np.sqrt(d_in_msg)
        inp['mb1'] = jnp.zeros((D_HID,), dtype=jnp.float32)
        inp['mW2'] = jax.random.normal(ks[5], (D_HID, D_NODE), dtype=jnp.float32) / np.sqrt(D_HID)
        inp['mb2'] = jnp.zeros((D_NODE,), dtype=jnp.float32)
        d_in_upd = 2 * D_NODE
        inp['uW1'] = jax.random.normal(ks[6], (d_in_upd, D_HID), dtype=jnp.float32) / np.sqrt(d_in_upd)
        inp['ub1'] = jnp.zeros((D_HID,), dtype=jnp.float32)
        inp['uW2'] = jax.random.normal(ks[7], (D_HID, D_NODE), dtype=jnp.float32) / np.sqrt(D_HID)
        inp['ub2'] = jnp.zeros((D_NODE,), dtype=jnp.float32)
        return inp
    _L0_gnn_all = _L0_gnn_setup()
    _L0_gnn_in = {k: v for k, v in _L0_gnn_all.items() if k in ('mW1', 'mb1', 'mW2', 'mb2', 'uW1', 'ub1', 'uW2', 'ub2')}
    del _L0_gnn_all

    def _L1_gnn_setup():
        import jax, jax.numpy as jnp
        import numpy as np
        N, E, D = (12500, 200000, 64)
        LN_EPS = 1e-05
        key = jax.random.key(seed)
        ks = jax.random.split(key, 8)
        x = jax.random.normal(ks[0], (N, D), dtype=jnp.float32)
        edge_index = jax.random.randint(ks[1], (2, E), 0, N, dtype=jnp.int64)
        edge_attr = jax.random.normal(ks[2], (E, D), dtype=jnp.float32)
        W1 = jax.random.normal(ks[3], (D, 2 * D), dtype=jnp.float32) / np.sqrt(D)
        b1 = jnp.zeros((2 * D,), dtype=jnp.float32)
        ln_g = jnp.ones((2 * D,), dtype=jnp.float32)
        ln_b = jnp.zeros((2 * D,), dtype=jnp.float32)
        W2 = jax.random.normal(ks[4], (2 * D, D), dtype=jnp.float32) / np.sqrt(2 * D)
        b2 = jnp.zeros((D,), dtype=jnp.float32)
        eps = jnp.zeros((1,), dtype=jnp.float32)
        return {'x': x, 'edge_index': edge_index, 'edge_attr': edge_attr, 'W1': W1, 'b1': b1, 'ln_g': ln_g, 'ln_b': ln_b, 'W2': W2, 'b2': b2, 'eps': eps}
    _L1_gnn_all = _L1_gnn_setup()
    _L1_gnn_in = {k: v for k, v in _L1_gnn_all.items() if k in ('W1', 'b1', 'ln_g', 'ln_b', 'W2', 'b2', 'eps')}
    del _L1_gnn_all

    def _L2_gnn_setup():
        import jax, jax.numpy as jnp
        import numpy as np
        V = 6250
        E = 100000
        D = 64
        key = jax.random.key(seed)
        ks = jax.random.split(key, 8)
        s = lambda fan_in: 1.0 / np.sqrt(fan_in)
        return {'vertices': jax.random.normal(ks[0], (V, D), dtype=jnp.float32), 'edges': jax.random.randint(ks[1], (2, E), 0, V, dtype=jnp.int64), 'ew1': jax.random.normal(ks[2], (2 * D, D), dtype=jnp.float32) * s(2 * D), 'eb1': jnp.zeros((D,), dtype=jnp.float32), 'ew2': jax.random.normal(ks[3], (D, D), dtype=jnp.float32) * s(D), 'eb2': jnp.zeros((D,), dtype=jnp.float32), 'vw1': jax.random.normal(ks[4], (2 * D, D), dtype=jnp.float32) * s(2 * D), 'vb1': jnp.zeros((D,), dtype=jnp.float32), 'vw2': jax.random.normal(ks[5], (D, D), dtype=jnp.float32) * s(D), 'vb2': jnp.zeros((D,), dtype=jnp.float32)}
    _L2_gnn_all = _L2_gnn_setup()
    _L2_gnn_in = {k: v for k, v in _L2_gnn_all.items() if k in ('ew1', 'eb1', 'ew2', 'eb2', 'vw1', 'vb1', 'vw2', 'vb2')}
    del _L2_gnn_all

    def _L3_gnn_setup():
        import jax, jax.numpy as jnp
        import numpy as np
        N_NODES = 6250
        N_EDGES = 200000
        NODE_DIM = 64
        EDGE_DIM = 32
        UNITS = 64

        def _glorot(key, shape):
            fan_in, fan_out = (shape[0], shape[1])
            lim = jnp.sqrt(6.0 / (fan_in + fan_out))
            return jax.random.uniform(key, shape, jnp.float32, -lim, lim)
        key = jax.random.key(seed)
        ks = jax.random.split(key, 16)
        msg_in = 2 * NODE_DIM + EDGE_DIM
        upd_in = NODE_DIM + UNITS
        return {'node_features': jax.random.normal(ks[0], (N_NODES, NODE_DIM), jnp.float32), 'edge_features': jax.random.normal(ks[1], (N_EDGES, EDGE_DIM), jnp.float32), 'senders': jax.random.randint(ks[2], (N_EDGES,), 0, N_NODES, jnp.int32), 'receivers': jnp.sort(jax.random.randint(ks[3], (N_EDGES,), 0, N_NODES, jnp.int32)), 'W1': _glorot(ks[4], (msg_in, UNITS)), 'b1': jnp.zeros((UNITS,), jnp.float32), 'W2': _glorot(ks[5], (UNITS, UNITS)), 'b2': jnp.zeros((UNITS,), jnp.float32), 'Wa1': _glorot(ks[6], (msg_in, UNITS)), 'ba1': jnp.zeros((UNITS,), jnp.float32), 'Wa2': _glorot(ks[7], (UNITS, 1)), 'ba2': jnp.zeros((1,), jnp.float32), 'Wu1': _glorot(ks[8], (upd_in, UNITS)), 'bu1': jnp.zeros((UNITS,), jnp.float32), 'Wu2': _glorot(ks[9], (UNITS, UNITS)), 'bu2': jnp.zeros((UNITS,), jnp.float32)}
    _L3_gnn_all = _L3_gnn_setup()
    _L3_gnn_in = {k: v for k, v in _L3_gnn_all.items() if k in ('W1', 'b1', 'W2', 'b2', 'Wa1', 'ba1', 'Wa2', 'ba2', 'Wu1', 'bu1', 'Wu2', 'bu2')}
    del _L3_gnn_all
    return {'x': x, 'src': src, 'dst': dst, 'edge_attr_32': edge_attr_32, 'edge_attr_64': edge_attr_64, 'L0_gnn_mW1': _L0_gnn_in['mW1'], 'L0_gnn_mb1': _L0_gnn_in['mb1'], 'L0_gnn_mW2': _L0_gnn_in['mW2'], 'L0_gnn_mb2': _L0_gnn_in['mb2'], 'L0_gnn_uW1': _L0_gnn_in['uW1'], 'L0_gnn_ub1': _L0_gnn_in['ub1'], 'L0_gnn_uW2': _L0_gnn_in['uW2'], 'L0_gnn_ub2': _L0_gnn_in['ub2'], 'L1_gnn_W1': _L1_gnn_in['W1'], 'L1_gnn_b1': _L1_gnn_in['b1'], 'L1_gnn_ln_g': _L1_gnn_in['ln_g'], 'L1_gnn_ln_b': _L1_gnn_in['ln_b'], 'L1_gnn_W2': _L1_gnn_in['W2'], 'L1_gnn_b2': _L1_gnn_in['b2'], 'L1_gnn_eps': _L1_gnn_in['eps'], 'L2_gnn_ew1': _L2_gnn_in['ew1'], 'L2_gnn_eb1': _L2_gnn_in['eb1'], 'L2_gnn_ew2': _L2_gnn_in['ew2'], 'L2_gnn_eb2': _L2_gnn_in['eb2'], 'L2_gnn_vw1': _L2_gnn_in['vw1'], 'L2_gnn_vb1': _L2_gnn_in['vb1'], 'L2_gnn_vw2': _L2_gnn_in['vw2'], 'L2_gnn_vb2': _L2_gnn_in['vb2'], 'L3_gnn_W1': _L3_gnn_in['W1'], 'L3_gnn_b1': _L3_gnn_in['b1'], 'L3_gnn_W2': _L3_gnn_in['W2'], 'L3_gnn_b2': _L3_gnn_in['b2'], 'L3_gnn_Wa1': _L3_gnn_in['Wa1'], 'L3_gnn_ba1': _L3_gnn_in['ba1'], 'L3_gnn_Wa2': _L3_gnn_in['Wa2'], 'L3_gnn_ba2': _L3_gnn_in['ba2'], 'L3_gnn_Wu1': _L3_gnn_in['Wu1'], 'L3_gnn_bu1': _L3_gnn_in['bu1'], 'L3_gnn_Wu2': _L3_gnn_in['Wu2'], 'L3_gnn_bu2': _L3_gnn_in['bu2']}

def reference(x, src, dst, edge_attr_32, edge_attr_64, L0_gnn_mW1, L0_gnn_mb1, L0_gnn_mW2, L0_gnn_mb2, L0_gnn_uW1, L0_gnn_ub1, L0_gnn_uW2, L0_gnn_ub2, L1_gnn_W1, L1_gnn_b1, L1_gnn_ln_g, L1_gnn_ln_b, L1_gnn_W2, L1_gnn_b2, L1_gnn_eps, L2_gnn_ew1, L2_gnn_eb1, L2_gnn_ew2, L2_gnn_eb2, L2_gnn_vw1, L2_gnn_vb1, L2_gnn_vw2, L2_gnn_vb2, L3_gnn_W1, L3_gnn_b1, L3_gnn_W2, L3_gnn_b2, L3_gnn_Wa1, L3_gnn_ba1, L3_gnn_Wa2, L3_gnn_ba2, L3_gnn_Wu1, L3_gnn_bu1, L3_gnn_Wu2, L3_gnn_bu2):
    import jax
    import jax.numpy as jnp

    def _L0_gnn_ref(nodes, row, col, edge_features, mW1, mb1, mW2, mb2, uW1, ub1, uW2, ub2):
        import jax, jax.numpy as jnp
        import numpy as np
        N_NODES = 6250
        N_EDGES = 100000
        D_NODE = 64
        D_EDGE = 32
        D_HID = 128

        def _mlp(x, W1, b1, W2, b2):
            return jax.nn.relu(x @ W1 + b1) @ W2 + b2
        msg_in = jnp.concatenate([nodes[row], nodes[col], edge_features], axis=-1)
        messages = _mlp(msg_in, mW1, mb1, mW2, mb2)
        aggregated = jax.ops.segment_sum(messages, col, num_segments=nodes.shape[0])
        upd_in = jnp.concatenate([nodes, aggregated], axis=-1)
        return _mlp(upd_in, uW1, ub1, uW2, ub2)

    def _L1_gnn_ref(x, edge_index, edge_attr, W1, b1, ln_g, ln_b, W2, b2, eps):
        import jax, jax.numpy as jnp
        import numpy as np
        N, E, D = (12500, 200000, 64)
        LN_EPS = 1e-05
        row, col = (edge_index[0], edge_index[1])
        message = jax.nn.relu(x[col] + edge_attr)
        message_reduce = jax.ops.segment_sum(message, row, num_segments=x.shape[0])
        h = (1.0 + eps) * x + jax.nn.relu(message_reduce)
        h1 = h @ W1 + b1
        mu = jnp.mean(h1, axis=-1, keepdims=True)
        var = jnp.mean(jnp.square(h1 - mu), axis=-1, keepdims=True)
        h1 = (h1 - mu) * jax.lax.rsqrt(var + LN_EPS) * ln_g + ln_b
        h1 = jax.nn.relu(h1)
        return h1 @ W2 + b2

    def _L2_gnn_ref(vertices, edges, ew1, eb1, ew2, eb2, vw1, vb1, vw2, vb2):
        import jax, jax.numpy as jnp
        import numpy as np
        V = 6250
        E = 100000
        D = 64
        src, dst = (edges[0], edges[1])
        edge_feat = jnp.concatenate([vertices[src], vertices[dst]], axis=-1)
        edge_feat = jnp.maximum(edge_feat @ ew1 + eb1, 0.0) @ ew2 + eb2
        aggregated = jnp.zeros_like(vertices).at[dst].add(edge_feat)
        combined = jnp.concatenate([vertices, aggregated], axis=-1)
        return jnp.maximum(combined @ vw1 + vb1, 0.0) @ vw2 + vb2

    def _L3_gnn_ref(node_features, edge_features, senders, receivers, W1, b1, W2, b2, Wa1, ba1, Wa2, ba2, Wu1, bu1, Wu2, bu2):
        import jax, jax.numpy as jnp
        import numpy as np
        N_NODES = 6250
        N_EDGES = 200000
        NODE_DIM = 64
        EDGE_DIM = 32
        UNITS = 64

        def _glorot(key, shape):
            fan_in, fan_out = (shape[0], shape[1])
            lim = jnp.sqrt(6.0 / (fan_in + fan_out))
            return jax.random.uniform(key, shape, jnp.float32, -lim, lim)
        act = jax.nn.swish
        msg_in = jnp.concatenate([node_features[senders], node_features[receivers], edge_features], axis=-1)
        messages = act(msg_in @ W1 + b1) @ W2 + b2
        att_logits = act(msg_in @ Wa1 + ba1) @ Wa2 + ba2
        att = jax.nn.softmax(att_logits, axis=0)
        messages = messages * att
        aggregated = jax.ops.segment_sum(messages, receivers, num_segments=node_features.shape[0])
        upd_in = jnp.concatenate([node_features, aggregated], axis=-1)
        return act(upd_in @ Wu1 + bu1) @ Wu2 + bu2
    edge_index = jnp.stack([src, dst])
    h = jnp.maximum(_layernorm(x, axis=-1), 0.0)
    x = x + _L0_gnn_ref(h, src, dst, edge_attr_32, L0_gnn_mW1, L0_gnn_mb1, L0_gnn_mW2, L0_gnn_mb2, L0_gnn_uW1, L0_gnn_ub1, L0_gnn_uW2, L0_gnn_ub2)
    h = jnp.maximum(_layernorm(x, axis=-1), 0.0)
    x = x + _L1_gnn_ref(h, edge_index, edge_attr_64, L1_gnn_W1, L1_gnn_b1, L1_gnn_ln_g, L1_gnn_ln_b, L1_gnn_W2, L1_gnn_b2, L1_gnn_eps)
    h = jnp.maximum(_layernorm(x, axis=-1), 0.0)
    x = x + _L2_gnn_ref(h, edge_index, L2_gnn_ew1, L2_gnn_eb1, L2_gnn_ew2, L2_gnn_eb2, L2_gnn_vw1, L2_gnn_vb1, L2_gnn_vw2, L2_gnn_vb2)
    h = jnp.maximum(_layernorm(x, axis=-1), 0.0)
    x = x + _L3_gnn_ref(h, edge_attr_32, src, dst, L3_gnn_W1, L3_gnn_b1, L3_gnn_W2, L3_gnn_b2, L3_gnn_Wa1, L3_gnn_ba1, L3_gnn_Wa2, L3_gnn_ba2, L3_gnn_Wu1, L3_gnn_bu1, L3_gnn_Wu2, L3_gnn_bu2)
    return x

_drawn_inputs = setup_inputs


def setup_inputs(seed=0):
    import zlib

    import numpy as np

    out = dict(_drawn_inputs(seed))
    spreads = {'L0_gnn_mb1': (0.0, 0.1),
     'L0_gnn_mb2': (0.0, 0.1),
     'L0_gnn_ub1': (0.0, 0.776),
     'L0_gnn_ub2': (0.0, 0.505),
     'L1_gnn_b1': (0.0, 2.0),
     'L1_gnn_ln_g': (1.0, 0.6),
     'L1_gnn_ln_b': (0.0, 0.8),
     'L1_gnn_b2': (0.0, 0.533),
     'L2_gnn_eb1': (0.0, 0.1),
     'L2_gnn_eb2': (0.0, 0.1),
     'L2_gnn_vb1': (0.0, 0.8),
     'L2_gnn_vb2': (0.0, 0.794),
     'L3_gnn_b1': (0.0, 2.0),
     'L3_gnn_b2': (0.0, 2.0),
     'L3_gnn_ba1': (0.0, 2.0),
     'L3_gnn_bu1': (0.0, 0.8),
     'L3_gnn_bu2': (0.0, 0.8)}
    factors = {'edge_attr_64': 4.478,
     'L3_gnn_W1': 25.53,
     'L3_gnn_W2': 8.0,
     'L3_gnn_Wa1': 8.0,
     'L3_gnn_Wa2': 8.0}
    for name, (base, spread) in spreads.items():
        noise = np.random.default_rng([zlib.crc32(name.encode()), seed]).standard_normal(out[name].shape)
        drawn = base * np.exp(spread * noise) if base else spread * noise
        out[name] = jnp.asarray(drawn.astype(out[name].dtype))
    for name, factor in factors.items():
        out[name] = (out[name] * factor).astype(out[name].dtype)
    return out
```

```python
import concourse.bass as bass
from concourse import mybir
from contextlib import ExitStack

F32 = mybir.dt.float32
I32 = mybir.dt.int32
ALU = mybir.AluOpType
ACT = mybir.ActivationFunctionType
AX = mybir.AxisListType

N_NODES, D, D_EDGE, HID = 6250, 64, 32, 128
N_EDGES = 200000
LN_EPS = 1e-5
P = 128
SUB = 4
GE = SUB * P
SLOTS = 4
GROUPS = -(-N_EDGES // (GE * SLOTS)) * SLOTS
ITERS = GROUPS // SLOTS
TILES = -(-N_NODES // P)
NPAD = TILES * P
WIN = 32
WINDOWS = NPAD // WIN
CT = 7
CHUNKS = TILES // CT
CN = CT * P
HALF = CN // 2
TABLES = 2 * SUB
LEAD = 3
GPC = GROUPS // 4
assert TABLES * CT * D <= (SLOTS + 3) * SUB * HID
assert GROUPS * WIN >= NPAD and SLOTS * SUB * (HID + 1) >= CT * 2 * HID and WIN + D_EDGE >= D
DST_AT = WIN + D_EDGE
SUM_ROW = (NPAD + P) * D // P // 5
assert TILES % CT == 0 and GROUPS % 4 == 0 and NPAD % WIN == 0 and NPAD > N_NODES


class Count:

    def __init__(self, sem):
        self.sem, self.base, self.per_pass, self.window = sem, 0, 0, None

    def begin(self, per_pass, window):
        self.per_pass, self.window = per_pass, window

    def end(self, passes):
        self.base += self.per_pass * passes

    def wait(self, eng, n):
        if isinstance(n, int) and n <= 0:
            return
        value = n + self.base
        if self.window is not None:
            value = self.window * self.per_pass + value
        eng.wait_ge(self.sem, value)


class Link:

    def __init__(self, eng, count):
        self.eng, self.count, self.n, self.inside = eng, count, 0, None

    def __call__(self, ins):
        self.n += 1
        ins.then_inc(self.count.sem, 1)
        if self.inside is None:
            self.count.wait(self.eng, self.n)
        else:
            i, first, each = self.inside
            self.count.wait(self.eng, (i - first) * each + self.n)

    def enter(self, i, first, each):
        self.inside, self.start = (i, first, each), self.n

    def leave(self, iterations):
        _, _, each = self.inside
        assert self.n - self.start == each, (self.n, self.start, each)
        self.inside, self.n = None, self.start + each * iterations

    def loop(self, eng, body, hold):
        before = self.n
        body(0)
        hold(eng)
        with eng.Fori(1, ITERS) as i:
            self.enter(i, 1, self.n - before)
            body(i)
            hold(eng)
        self.leave(ITERS - 1)


def gnn(nc, t, out):
    ctx = ExitStack()
    with ctx:
        _gnn(nc, t, out, ctx)


def _gnn(nc, t, out, ctx):
    def sb(name, shape, dt=F32):
        return ctx.enter_context(nc.sbuf_tensor(name, shape, dt))

    def sem(name):
        return ctx.enter_context(nc.semaphore(name))

    def dram(name, shape, dt=F32):
        return nc.dram_tensor(name, shape, dt, kind="Internal").ap()

    x_all = sb("x_all", [P, TILES * D])
    h_all = sb("h_all", [P, TILES * D])
    hT = sb("hT", [D + 1, NPAD])
    acc = sb("acc", [P, NPAD])
    parts = sb("parts", [D + 1, GROUPS * WIN])
    deg = parts[0:1, 0:NPAD]
    dst_i = sb("dst_i", [P, GROUPS * SUB], I32)
    dst_rel = sb("dst_rel", [P, GROUPS * SUB])
    base_row = sb("base_row", [1, GROUPS], I32)
    base_cols = sb("base_col", [DST_AT + WIN, GROUPS])
    base_col = base_cols[DST_AT:DST_AT + WIN, :]
    win_id = sb("win_id", [P, 1])
    ident = sb("ident", [P, P])
    earlier = sb("earlier", [P, P])
    iota_w = sb("iota_w", [P, WIN])
    place = sb("place", [P, 1])
    dummy = sb("dummy_row", [P, 1])
    ones_c = sb("ones_c", [P, 1])
    ones_r = sb("ones_r", [P, P])
    eps_c = sb("eps_c", [P, 1])
    idx = [sb(f"idx{q}", [P, SUB], I32) for q in range(SLOTS)]
    stack_all = sb("stack_all", [DST_AT + WIN, SLOTS * GE])
    dst_b = [stack_all[DST_AT:DST_AT + WIN, q * GE:(q + 1) * GE].bitcast(I32) for q in range(SLOTS)]
    stack = [stack_all[:, q * GE:(q + 1) * GE] for q in range(SLOTS)]
    rows = [sb(f"rows{q}", [WIN + D_EDGE, HID]) for q in range(SLOTS)]
    onehot = [sb(f"onehot{q}", [P, SUB * WIN]) for q in range(SLOTS)]
    scratch = sb("scratch", [P, (SLOTS + 3) * SUB * HID])
    z = [scratch[:, q * SUB * HID:(q + 1) * SUB * HID] for q in range(SLOTS)]
    msg_all = sb("msg_all", [P, SLOTS * SUB * (HID + 1)])
    msg = [msg_all[:, q * SUB * (HID + 1):(q + 1) * SUB * (HID + 1)] for q in range(SLOTS)]
    half = [scratch[:, (SLOTS + b) * SUB * HID:(SLOTS + b + 1) * SUB * HID] for b in range(2)]
    prod = scratch[:, (SLOTS + 2) * SUB * HID:]
    logit = [sb(f"logit{b}", [P, SUB]) for b in range(2)]
    gmax = [sb(f"gmax{b}", [P, 1]) for b in range(2)]
    gmax1 = [sb(f"gmax1{b}", [1, 1]) for b in range(2)]
    nmax = [sb(f"nmax{b}", [P, 1]) for b in range(2)]
    prob = [sb(f"prob{b}", [P, SUB]) for b in range(2)]
    gmax_row = sb("gmax_row", [1, GROUPS])
    scale_row = sb("scale_row", [1, GROUPS])
    tot = sb("tot", [D + 1, 2])
    itot = sb("itot", [D, 1])
    gm1 = sb("gm1", [1, 2])
    dup = sb("dup", [P, 4 * SUB])
    equal = [half[b][:, :] for b in range(2)]
    src_b = [acc[:, q * GE:(q + 1) * GE].bitcast(I32) for q in range(SLOTS)]
    comb = [acc[:, SLOTS * GE + q * SUB * D:SLOTS * GE + (q + 1) * SUB * D] for q in range(SLOTS)]
    idx_e = [sb(f"idx_e{q}", [P, SUB], I32) for q in range(SLOTS)]
    hTc = sb("hTc", [D + 1, CN])
    aggT = stack_all[0:D, 0:CN]
    u1T = sb("u1T", [HID, CN])
    pq = msg_all[:, 0:CT * 2 * HID]
    xm = sb("xm", [P, CT * HID])
    sq = sb("sq", [P, CT * HID])
    st = sb("st", [P, 4 * CT])
    tabs = [scratch[:, k * CT * D:(k + 1) * CT * D] for k in range(TABLES)]
    zero_row = sb("zero_row", [P, SUM_ROW])
    w_pq = [sb(f"w_pq{l}", [D + 1, 2 * HID]) for l in (0, 2, 3)]
    w_pq = {0: w_pq[0], 2: w_pq[1], 3: w_pq[2]}
    w_agg = {l: sb(f"w_agg{l}", [HID if l == 0 else D + 1, P]) for l in (0, 2, 3)}
    b_agg = {l: sb(f"b_agg{l}", [1, P]) for l in (0, 2)}
    w_u1h = {l: sb(f"w_u1h{l}", [D + 1, HID]) for l in (0, 1, 2, 3)}
    w_u1a = {l: sb(f"w_u1a{l}", [D, HID]) for l in (0, 2, 3)}
    w_u2 = {l: sb(f"w_u2{l}", [HID, D]) for l in (0, 1, 2, 3)}
    b_u2 = {l: sb(f"b_u2{l}", [1, D]) for l in (0, 1, 2, 3)}
    ln_gb = sb("ln_gb", [P, 2 * HID])
    eps1 = sb("eps1", [P, 1])
    wa2 = sb("wa2", [P, D])
    ba2 = sb("ba2", [P, 1])
    bank = [ctx.enter_context(nc.psum_tensor(f"bank{i}", [P, 512], F32)) for i in range(8)]

    hid_of = {0: HID, 2: D, 3: HID}
    p_tab = {l: dram(f"p_tab{l}", (NPAD, hid_of[l])) for l in (0, 2, 3)}
    q_tab = {l: dram(f"q_tab{l}", (NPAD, hid_of[l])) for l in (0, 2, 3)}
    h_tab = dram("h_tab", (NPAD, D))
    sums = [dram(f"sums{k}", (NPAD + P, D)) for k in range(TABLES)]
    base_d = dram("base_d", (GROUPS,), I32)
    span_d = dram("span_d", (GROUPS,), I32)

    s_const, s_w, s_dst, s_dc, s_bd, s_bb = (sem(n) for n in (
        "constants_made", "weights_in", "dst_in", "index_steps", "bases_out", "bases_in"))
    s_zero, s_zt = sem("x_zeroed"), sem("sums_zeroed")
    CONSTS = 13
    weights = []
    for l, w1, b1 in ((0, "L0_gnn_mW1", "L0_gnn_mb1"), (2, "L2_gnn_ew1", "L2_gnn_eb1")):
        h = hid_of[l]
        weights += [(w_pq[l][0:D, 0:h], t[w1][0:D, :]), (w_pq[l][0:D, h:2 * h], t[w1][D:2 * D, :]),
                    (w_pq[l][D:D + 1, h:2 * h], t[b1][None, :])]
    for o, w1, b1 in ((0, "L3_gnn_Wa1", "L3_gnn_ba1"), (D, "L3_gnn_W1", "L3_gnn_b1")):
        weights += [(w_pq[3][0:D, o:o + D], t[w1][0:D, :]), (w_pq[3][0:D, HID + o:HID + o + D], t[w1][D:2 * D, :]),
                    (w_pq[3][D:D + 1, HID + o:HID + o + D], t[b1][None, :])]
    weights += [(w_agg[0][:, 0:D], t["L0_gnn_mW2"]), (w_agg[2][0:D, 0:D], t["L2_gnn_ew2"]),
                (w_agg[3][0:D, 0:D], t["L3_gnn_W2"]), (w_agg[3][D:D + 1, 0:D], t["L3_gnn_b2"][None, :]),
                (b_agg[0][:, 0:D], t["L0_gnn_mb2"][None, :]), (b_agg[2][:, 0:D], t["L2_gnn_eb2"][None, :])]
    for l, w1, b1, w2, b2 in ((0, "L0_gnn_uW1", "L0_gnn_ub1", "L0_gnn_uW2", "L0_gnn_ub2"),
                              (1, "L1_gnn_W1", "L1_gnn_b1", "L1_gnn_W2", "L1_gnn_b2"),
                              (2, "L2_gnn_vw1", "L2_gnn_vb1", "L2_gnn_vw2", "L2_gnn_vb2"),
                              (3, "L3_gnn_Wu1", "L3_gnn_bu1", "L3_gnn_Wu2", "L3_gnn_bu2")):
        h = t[w1].shape[1]
        weights += [(w_u1h[l][0:D, 0:h], t[w1][0:D, :]), (w_u1h[l][D:D + 1, 0:h], t[b1][None, :]),
                    (w_u2[l][0:h, :], t[w2]), (b_u2[l][:, :], t[b2][None, :])]
        if l != 1:
            weights += [(w_u1a[l][:, 0:h], t[w1][D:2 * D, :])]
    weights += [(ln_gb[:, 0:HID], t["L1_gnn_ln_g"][None, :].to_broadcast((P, HID))),
                (ln_gb[:, HID:2 * HID], t["L1_gnn_ln_b"][None, :].to_broadcast((P, HID))),
                (eps1[:, :], t["L1_gnn_eps"][None, :].to_broadcast((P, 1))),
                (wa2[:, :], t["L3_gnn_Wa2"].rearrange("d a -> a d").to_broadcast((P, D))),
                (ba2[:, :], t["L3_gnn_ba2"][None, :].to_broadcast((P, 1)))]
    for q in range(SLOTS):
        weights += [(rows[q][WIN:WIN + D_EDGE, 0:HID], t["L0_gnn_mW1"][2 * D:2 * D + D_EDGE, :])]
    whole = N_NODES // P
    rest = N_NODES - whole * P
    base_b = half[0][:, 0:GROUPS].bitcast(I32)
    gcols = [zz[0:GPC, :].bitcast(I32) for zz in z]
    bmin, bmax = st[0:GPC, 0:4], st[0:GPC, 4:8]
    bint = idx_e[0][0:GPC, :]
    sint = idx_e[1][0:GPC, :]

    with nc.Block() as block:
        @block.gpsimd
        def _(pool):
            nc.gpsimd.memset(ident[:, :], 0.0).then_inc(s_const, 1)
            nc.gpsimd.memset(earlier[:, :], 1.0).then_inc(s_const, 1)
            pool.wait_ge(s_const, 2)
            nc.gpsimd.affine_select(out=ident[:, :], in_=ident[:, :], compare_op=ALU.not_equal, fill=1.0,
                                    base=0, pattern=[[-1, P]], channel_multiplier=1).then_inc(s_const, 1)
            nc.gpsimd.affine_select(out=earlier[:, :], in_=earlier[:, :], compare_op=ALU.is_gt, fill=0.0,
                                    base=0, pattern=[[-1, P]], channel_multiplier=1).then_inc(s_const, 1)
            nc.gpsimd.iota(iota_w[:, :], pattern=[[1, WIN]], base=0, channel_multiplier=0,
                           allow_small_or_imprecise_dtypes=True).then_inc(s_const, 1)
            nc.gpsimd.iota(place[:, :], pattern=[[1, 1]], base=-DST_AT, channel_multiplier=1,
                           allow_small_or_imprecise_dtypes=True).then_inc(s_const, 1)
            nc.gpsimd.iota(dummy[:, :], pattern=[[1, 1]], base=NPAD, channel_multiplier=1,
                           allow_small_or_imprecise_dtypes=True).then_inc(s_const, 1)
            for tile, value in ((ones_c, 1.0), (ones_r, 1.0), (eps_c, LN_EPS), (acc, 0.0), (zero_row, 0.0), (deg, 0.0)):
                nc.gpsimd.memset(tile if tile is deg else tile[:, :], value).then_inc(s_const, 1)
            pool.wait_ge(s_const, CONSTS)

        @block.sync
        def _(sp):
            for c in range(4):
                sp.dma_start(gcols[c], t["dst_groups"].rearrange("(p c) e -> c p e", c=4)[c]).then_inc(s_dst, 16)
            sp.dma_start(dst_i[:, :].rearrange("p (g j) -> p g j", j=SUB),
                         t["dst_tiles"]).then_inc(s_dst, 16)
            sp.wait_ge(s_dc, 11)
            sp.dma_start(base_d.rearrange("(p c) -> p c", c=4), bint).then_inc(s_bd, 16)
            sp.dma_start(span_d.rearrange("(p c) -> p c", c=4), sint).then_inc(s_bd, 16)
            sp.wait_ge(s_bd, 32)
            sp.dma_start(base_row[:, :], base_d[None, :]).then_inc(s_bb, 16)
            sp.dma_start(gmax_row[:, :].bitcast(I32), span_d[None, :]).then_inc(s_bb, 16)
            sp.dma_start(base_b, base_d[None, :].to_broadcast((P, GROUPS))).then_inc(s_bb, 16)
            sp.wait_ge(s_const, CONSTS)
            for k in range(TABLES):
                sp.dma_start(sums[k].rearrange("(p a r) d -> p a (r d)", p=P, a=5),
                             zero_row[:, None, :].to_broadcast((P, 5, SUM_ROW))).then_inc(s_zt, 16)
            sp.wait_ge(s_bb, 48)
            sp.wait_ge(s_zt, 16 * TABLES)

        @block.scalar
        def _(act):
            xv = x_all[:, :].rearrange("p (t d) -> p t d", d=D)
            act.wait_ge(s_zero, 1)
            act.dma_start(xv[:, 0:whole, :],
                          t["x"][0:whole * P, :].rearrange("(t p) d -> p t d", p=P)).then_inc(s_w, 16)
            act.dma_start(xv[0:rest, whole, :], t["x"][whole * P:N_NODES, :]).then_inc(s_w, 16)
            with nc.allow_non_contiguous_dma(reason="a column of weights"):
                for to, of in weights:
                    act.dma_start(to, of).then_inc(s_w, 16)
            act.wait_ge(s_w, 16 * (len(weights) + 2))

        @block.vector
        def _(dve):
            nc.vector.memset(x_all[:, :], 0.0).then_inc(s_zero, 1)
            nc.vector.memset(hT[D:D + 1, :], 1.0).then_inc(s_zero, 1)
            nc.vector.memset(hTc[D:D + 1, :], 1.0).then_inc(s_zero, 1)
            for w in (w_agg[0], w_agg[2], w_agg[3], b_agg[0], b_agg[2]):
                nc.vector.memset(w[:, D:P], 0.0).then_inc(s_zero, 1)
            for l in (0, 2, 3):
                nc.vector.memset(w_pq[l][D:D + 1, 0:hid_of[l]], 0.0).then_inc(s_zero, 1)
            dve.wait_ge(s_dst, 80)
            for c in range(4):
                nc.vector.tensor_reduce(bmin[:, c:c + 1], gcols[c], AX.X, ALU.min).then_inc(s_dc, 1)
                nc.vector.tensor_reduce(bmax[:, c:c + 1], gcols[c], AX.X, ALU.max).then_inc(s_dc, 1)
            dve.wait_ge(s_dc, 8)
            nc.vector.tensor_scalar(bmin, bmin, float(NPAD - WIN), None, ALU.min).then_inc(s_dc, 1)
            dve.wait_ge(s_dc, 9)
            nc.vector.tensor_copy(bint, bmin).then_inc(s_dc, 1)
            nc.vector.tensor_tensor(sint, bmax, bmin, ALU.subtract).then_inc(s_dc, 1)
            dve.wait_ge(s_bb, 48)
            dve.wait_ge(s_const, CONSTS)
            nc.vector.tensor_scalar(base_col, base_b[DST_AT:DST_AT + WIN, :], place[DST_AT:DST_AT + WIN, 0:1], None,
                                    ALU.add).then_inc(s_dc, 1)
            nc.vector.tensor_tensor(dst_rel[:, :].rearrange("p (g j) -> p g j", j=SUB),
                                    dst_i[:, :].rearrange("p (g j) -> p g j", j=SUB),
                                    base_b[:, :, None].to_broadcast((P, GROUPS, SUB)),
                                    ALU.subtract).then_inc(s_dc, 1)
            nc.vector.tensor_reduce(gm1[:, 0:1], gmax_row[:, :].bitcast(I32), AX.X, ALU.max).then_inc(s_dc, 1)
            dve.wait_ge(s_dc, 14)
            nc.vector.tensor_copy(gm1[:, 1:2].bitcast(I32), gm1[:, 0:1]).then_inc(s_dc, 1)
            dve.wait_ge(s_w, 16 * (len(weights) + 2))
            nc.vector.tensor_scalar(wa2[:, :], wa2[:, :], 0.5, None, ALU.mult).then_inc(s_dc, 1)
            nc.vector.tensor_scalar(w_agg[3][0:D, :], w_agg[3][0:D, :], 0.5, None, ALU.mult).then_inc(s_dc, 1)
            nc.vector.tensor_scalar(w_u2[3][0:D, :], w_u2[3][0:D, :], 0.5, None, ALU.mult).then_inc(s_dc, 1)
            nc.vector.memset(win_id[:, :], -float(WIN)).then_inc(s_dc, 1)
            nc.vector.tensor_scalar(eps1[:, :], eps1[:, :], 1.0, None, ALU.add).then_inc(s_dc, 1)
            dve.wait_ge(s_dc, 20)

    widest = nc.values_load(gm1[0:1, 1:2].bitcast(I32), min_val=0, max_val=NPAD)

    def hold(eng):
        eng.sem_inc(s_held, 1)

    class Stage:

        def __init__(self, name, by=1):
            self.sem, self.by, self.base = sem(name), by, 0

        def wait(self, eng, i, before=0):
            if isinstance(i, int) and i < before:
                return
            eng.wait_ge(self.sem, (i - before + 1) * self.by + self.base)

        def end(self):
            self.base += self.by * CHUNKS

    agg, agg_out, hidden, hidden_tanh, hidden_out, y_done, x_new = (Stage(n) for n in (
        "agg", "agg_out", "hidden", "hidden_tanh", "hidden_out", "y_done", "x_new"))
    tab_in, mix, mixT, mixT_out, h1, var1, std1, h1n, h1T = (Stage(n, b) for n, b in (
        ("tab_in", 16 * TABLES), ("mix", 1), ("mixT", 1), ("mixT_out", 1), ("h1", 1), ("var1", 1), ("std1", 1),
        ("h1n", 1), ("h1T", 1)))
    var, std, h_ready, trans, trans_out, pq_ready, pq_out = (Stage(n) for n in (
        "var", "std", "h_ready", "trans", "trans_out", "pq_ready", "pq_out"))
    pq_stored, h_stored, x_stored = Stage("pq_stored", 32), Stage("h_stored", 16), Stage("x_stored", 16)
    s_tot, s_totb, s_acc0 = sem("total"), sem("total_spread"), sem("acc_zeroed")
    s_vec = sem("vector_steps")
    vec = [0]

    def pieces(width):
        return ((0, 0, 4 * width), (1, 4 * width, (CT - 4) * width))

    def node_phase(done, coming):
        hu = {0: HID, 1: HID, 2: D, 3: D}.get(done)
        hp = hid_of.get(coming)
        makes_pq = coming in (0, 2, 3)
        live = []
        if done in (0, 2, 3):
            live += [agg, agg_out, hidden] + [hidden_tanh] * (done == 3)
        if done == 1:
            live += [tab_in, mix, mixT, mixT_out, h1, var1, std1, h1n, h1T]
        if done is not None:
            live += [hidden_out, y_done, x_new]
        if coming is not None:
            live += [var, std, h_ready]
        if makes_pq:
            live += [trans, trans_out, pq_ready, pq_out, pq_stored]
        if coming == 1:
            live += [h_stored]
        if coming is None:
            live += [x_stored]

        def run(eng, chunk):
            chunk(0)
            with eng.Fori(1, CHUNKS) as i:
                chunk(i)

        with nc.Block() as block:
            @block.tensor
            def _(pe):
                def transposes(src, width, banks, n):
                    hold(pe)
                    for k in range(CT):
                        mm = nc.tensor.transpose(bank[banks + k // 4][0:width, k % 4 * P:(k % 4 + 1) * P],
                                                 src[:, k * width:(k + 1) * width], ident[:, :])
                    mm.then_inc(n.sem, 1)

                def chunk(i):
                    if done in (0, 2, 3):
                        k = {0: HID, 2: D, 3: D + 1}[done]
                        agg_out.wait(pe, i, before=1)
                        if makes_pq:
                            trans_out.wait(pe, i, before=1)
                        for b in range(2):
                            at = bass.ds(i * CN + b * HALF, HALF)
                            mm = nc.tensor.matmul(bank[b][:, 0:HALF], w_agg[done][0:k, :], acc[0:k, at],
                                                  start=True, stop=done == 3)
                            if done != 3:
                                mm = nc.tensor.matmul(bank[b][:, 0:HALF], b_agg[done][:, :], deg[:, at],
                                                      start=False, stop=True)
                        mm.then_inc(agg.sem, 1)
                        hidden_out.wait(pe, i, before=1)
                        if makes_pq:
                            pq_out.wait(pe, i, before=1)
                        agg_out.wait(pe, i)
                        for b in range(2):
                            nc.tensor.matmul(bank[2 + b][0:hu, 0:HALF], w_u1h[done][:, 0:hu],
                                             hT[:, bass.ds(i * CN + b * HALF, HALF)], start=True, stop=False)
                            mm = nc.tensor.matmul(bank[2 + b][0:hu, 0:HALF], w_u1a[done][:, 0:hu],
                                                  aggT[:, b * HALF:(b + 1) * HALF], start=False, stop=True)
                        mm.then_inc(hidden.sem, 1)
                    if done == 1:
                        trans_out.wait(pe, i, before=1)
                        mix.wait(pe, i)
                        transposes(xm, D, 0, mixT)
                        mixT_out.wait(pe, i)
                        pq_out.wait(pe, i, before=1)
                        for k in range(CT):
                            mm = nc.tensor.matmul(bank[2 + k // 4][:, k % 4 * P:(k % 4 + 1) * P],
                                                  hTc[:, k * P:(k + 1) * P], w_u1h[1][:, :], start=True, stop=True)
                        mm.then_inc(h1.sem, 1)
                        h1n.wait(pe, i)
                        transposes(sq, HID, 5, h1T)
                    if done is not None:
                        hidden_out.wait(pe, i)
                        x_new.wait(pe, i, before=1)
                        for k in range(CT):
                            nc.tensor.matmul(bank[4][:, k * D:(k + 1) * D], u1T[0:hu, k * P:(k + 1) * P],
                                             w_u2[done][0:hu, :], start=True, stop=False)
                            mm = nc.tensor.matmul(bank[4][:, k * D:(k + 1) * D], ones_r[0:1, :], b_u2[done][:, :],
                                                  start=False, stop=True)
                        mm.then_inc(y_done.sem, 1)
                    if makes_pq:
                        trans_out.wait(pe, i, before=1)
                        h_ready.wait(pe, i)
                        transposes(xm, D, 0, trans)
                        trans_out.wait(pe, i)
                        pq_out.wait(pe, i, before=1)
                        for k in range(CT):
                            b = (2, 3, 5, 6)[k // 2]
                            mm = nc.tensor.matmul(bank[b][:, k % 2 * 2 * hp:(k % 2 + 1) * 2 * hp],
                                                  hTc[:, k * P:(k + 1) * P], w_pq[coming][:, 0:2 * hp],
                                                  start=True, stop=True)
                        mm.then_inc(pq_ready.sem, 1)

                if done == 3:
                    pe.wait_ge(s_tot, 1)
                    nc.tensor.matmul(bank[7][0:D, 0:1], ones_r[D:D + 1, 0:D], tot[D:D + 1, 0:1],
                                     start=True, stop=True).then_inc(s_totb, 1)
                run(pe, chunk)

            @block.scalar
            def _(act):
                def chunk(i):
                    if done in (0, 2, 3):
                        hidden.wait(act, i, before=1)
                        agg.wait(act, i)
                        for b in range(2):
                            a = nc.scalar.activation(aggT[:, b * HALF:(b + 1) * HALF], bank[b][0:D, 0:HALF],
                                                     ACT.Copy, scale=itot[:, 0:1] if done == 3 else 1.0)
                        a.then_inc(agg_out.sem, 1)
                        hidden.wait(act, i)
                        y_done.wait(act, i, before=1)
                        if done == 3:
                            for b in range(2):
                                a = nc.scalar.activation(xm[0:D, b * HALF:(b + 1) * HALF],
                                                         bank[2 + b][0:D, 0:HALF], ACT.Tanh, scale=0.5)
                            a.then_inc(hidden_tanh.sem, 1)
                        else:
                            for b in range(2):
                                a = nc.scalar.activation(u1T[0:hu, b * HALF:(b + 1) * HALF],
                                                         bank[2 + b][0:hu, 0:HALF], ACT.Relu)
                            a.then_inc(hidden_out.sem, 1)
                    if done == 1:
                        pq_ready.wait(act, i, before=1)
                        mixT.wait(act, i)
                        for b, c, w in pieces(P):
                            a = nc.scalar.activation(hTc[0:D, c:c + w], bank[b][0:D, 0:w], ACT.Copy)
                        a.then_inc(mixT_out.sem, 1)
                        var1.wait(act, i)
                        nc.scalar.activation(st[:, CT:2 * CT], st[:, 0:CT], ACT.Sqrt, bias=eps_c[:, 0:1],
                                             scale=1.0 / HID).then_inc(std1.sem, 1)
                        y_done.wait(act, i, before=1)
                        h1T.wait(act, i)
                        for b, c, w in pieces(P):
                            a = nc.scalar.activation(u1T[:, c:c + w], bank[5 + b][:, 0:w], ACT.Relu)
                        a.then_inc(hidden_out.sem, 1)
                    if coming is not None:
                        var.wait(act, i)
                        nc.scalar.activation(st[:, CT:2 * CT], st[:, 0:CT], ACT.Sqrt, bias=eps_c[:, 0:1],
                                             scale=1.0 / D).then_inc(std.sem, 1)
                    if makes_pq:
                        pq_ready.wait(act, i, before=1)
                        trans.wait(act, i)
                        for b, c, w in pieces(P):
                            nc.scalar.activation(hT[0:D, bass.ds(i * CN + c, w)], bank[b][0:D, 0:w], ACT.Copy)
                            a = nc.scalar.activation(hTc[0:D, c:c + w], bank[b][0:D, 0:w], ACT.Copy)
                        a.then_inc(trans_out.sem, 1)
                        pq_stored.wait(act, i, before=1)
                        pq_ready.wait(act, i)
                        for k in range(4):
                            w = min(2, CT - 2 * k) * 2 * hp
                            a = nc.scalar.activation(pq[:, k * 4 * hp:k * 4 * hp + w],
                                                     bank[(2, 3, 5, 6)[k]][:, 0:w], ACT.Copy)
                        a.then_inc(pq_out.sem, 1)

                if done == 3:
                    act.wait_ge(s_tot, 2)
                run(act, chunk)

            @block.vector
            def _(dve):
                base, per, at = vec[0], [0], [0]

                def link(i, ins):
                    at[0] += 1
                    ins.then_inc(s_vec, 1)
                    dve.wait_ge(s_vec, i * per[0] + base + at[0])

                def deviations(i, width, source, ready):
                    m3 = xm[:, 0:CT * width].rearrange("p (c d) -> p c d", d=width)
                    q3 = sq[:, 0:CT * width].rearrange("p (c d) -> p c d", d=width)
                    mean = st[:, 2 * CT:3 * CT]
                    hold(dve)
                    for c0, c1, s3 in source:
                        link(i, nc.vector.tensor_reduce(mean[:, c0:c1], s3, AX.X, ALU.add))
                    link(i, nc.vector.tensor_scalar(mean, mean, 1.0 / width, None, ALU.mult))
                    for c0, c1, s3 in source:
                        link(i, nc.vector.tensor_tensor(
                            m3[:, c0:c1, :], s3, mean[:, c0:c1, None].to_broadcast((P, c1 - c0, width)),
                            ALU.subtract))
                    link(i, nc.vector.tensor_tensor(q3, m3, m3, ALU.mult))
                    nc.vector.tensor_reduce(st[:, 0:CT], q3, AX.X, ALU.add).then_inc(ready.sem, 1)
                    return m3, q3

                def scale_rows(i, m3, width):
                    link(i, nc.vector.reciprocal(st[:, 3 * CT:4 * CT], st[:, CT:2 * CT]))
                    link(i, nc.vector.tensor_tensor(
                        m3, m3, st[:, 3 * CT:4 * CT, None].to_broadcast((P, CT, width)), ALU.mult))

                def chunk(i):
                    at[0] = 0
                    w = CT * D
                    if done == 3:
                        hidden_tanh.wait(dve, i)
                        for b in range(2):
                            a = nc.vector.scalar_tensor_tensor(
                                u1T[0:D, b * HALF:(b + 1) * HALF], xm[0:D, b * HALF:(b + 1) * HALF], 1.0,
                                bank[2 + b][0:D, 0:HALF], ALU.add, ALU.mult)
                        a.then_inc(hidden_out.sem, 1)
                    if done == 1:
                        tab_in.wait(dve, i)
                        link(i, nc.vector.tensor_tensor(sq[:, 0:w], tabs[0], tabs[1], ALU.add))
                        for k in range(2, TABLES):
                            link(i, nc.vector.tensor_tensor(sq[:, 0:w], sq[:, 0:w], tabs[k], ALU.add))
                        link(i, nc.vector.tensor_scalar(sq[:, 0:w], sq[:, 0:w], 0.0, None, ALU.max))
                        link(i, nc.vector.tensor_scalar(xm[:, 0:w], h_all[:, bass.ds(i * w, w)], eps1[:, 0:1], None,
                                                        ALU.mult))
                        nc.vector.tensor_tensor(xm[:, 0:w], xm[:, 0:w], sq[:, 0:w], ALU.add).then_inc(mix.sem, 1)
                        h1.wait(dve, i)
                        m3, q3 = deviations(i, HID, [
                            (0, 4, bank[2][:, 0:4 * HID].rearrange("p (c d) -> p c d", d=HID)),
                            (4, CT, bank[3][:, 0:(CT - 4) * HID].rearrange("p (c d) -> p c d", d=HID))], var1)
                        std1.wait(dve, i)
                        scale_rows(i, m3, HID)
                        link(i, nc.vector.tensor_tensor(m3, m3, ln_gb[:, None, 0:HID].to_broadcast((P, CT, HID)),
                                                        ALU.mult))
                        nc.vector.tensor_tensor(q3, m3, ln_gb[:, None, HID:2 * HID].to_broadcast((P, CT, HID)),
                                                ALU.add).then_inc(h1n.sem, 1)
                    xc = x_all[:, bass.ds(i * w, w)]
                    if done is not None:
                        y_done.wait(dve, i)
                        nc.vector.tensor_tensor(xc, xc, bank[4][:, 0:w], ALU.add).then_inc(x_new.sem, 1)
                        x_new.wait(dve, i)
                    if coming is not None:
                        if coming == 1:
                            h_stored.wait(dve, i, before=1)
                        m3, q3 = deviations(i, D, [(0, CT, xc.rearrange("p (c d) -> p c d", d=D))], var)
                        std.wait(dve, i)
                        scale_rows(i, m3, D)
                        nc.vector.tensor_scalar(xm[:, 0:w], xm[:, 0:w], 0.0, None, ALU.max).then_inc(h_ready.sem, 1)
                        h_ready.wait(dve, i)
                        if coming == 1:
                            link(i, nc.vector.tensor_copy(h_all[:, bass.ds(i * w, w)], xm[:, 0:w]))
                        else:
                            trans.wait(dve, i)
                    per[0] = at[0]
                    hold(dve)

                if done == 3:
                    nc.vector.tensor_reduce(tot[D:D + 1, 0:1], acc[D:D + 1, 0:N_NODES], AX.X,
                                            ALU.add).then_inc(s_tot, 1)
                    dve.wait_ge(s_totb, 1)
                    nc.vector.reciprocal(itot[:, :], bank[7][0:D, 0:1]).then_inc(s_tot, 1)
                run(dve, chunk)
                vec[0] += per[0] * CHUNKS
                if coming in (2, 3):
                    nc.vector.memset(acc[:, :], 0.0).then_inc(s_acc0, 1)
                if coming == 3:
                    pq_stored.wait(dve, CHUNKS - 1)
                    for q in range(SLOTS):
                        nc.vector.memset(msg[q].rearrange("p (j h) -> p j h", h=HID + 1)[:, :, HID:HID + 1], 1.0)\
                            .then_inc(s_acc0, 1)

            @block.sync
            def _(sp):
                if coming == 3:
                    for q in range(SLOTS):
                        for o, w1 in ((0, "L3_gnn_Wa1"), (D, "L3_gnn_W1")):
                            sp.dma_start(rows[q][WIN:WIN + D_EDGE, o:o + D], t[w1][2 * D:2 * D + D_EDGE, :])\
                                .then_inc(s_w3, 16)
                    sp.wait_ge(s_w3, 16 * 2 * SLOTS)

                def chunk(i):
                    tiles = bass.ds(i * CT, CT)
                    if done == 1:
                        mix.wait(sp, i, before=1)
                        for k in range(TABLES):
                            sp.dma_start(tabs[k].rearrange("p (c d) -> p c d", d=D),
                                         sums[k][0:NPAD, :].rearrange("(t p) d -> p t d", p=P)[:, tiles, :])\
                                .then_inc(tab_in.sem, 16)
                    if makes_pq:
                        pq_out.wait(sp, i)
                        v = pq[:, 0:CT * 2 * hp].rearrange("p (c h) -> p c h", h=2 * hp)
                        for tab, c in ((p_tab[coming], 0), (q_tab[coming], hp)):
                            sp.dma_start(tab.rearrange("(t p) h -> p t h", p=P)[:, tiles, :],
                                         v[:, :, c:c + hp]).then_inc(pq_stored.sem, 16)
                    if coming == 1:
                        h_ready.wait(sp, i)
                        sp.dma_start(h_tab.rearrange("(t p) d -> p t d", p=P)[:, tiles, :],
                                     xm[:, 0:CT * D].rearrange("p (c d) -> p c d", d=D)).then_inc(h_stored.sem, 16)

                run(sp, chunk) if done == 1 or coming is not None else None
                if makes_pq:
                    pq_stored.wait(sp, CHUNKS - 1)
                if coming == 1:
                    h_stored.wait(sp, CHUNKS - 1)
                if coming is None:
                    x_new.wait(sp, CHUNKS - 1)
                    xv = x_all[:, :].rearrange("p (t d) -> p t d", d=D)
                    sp.dma_start(out[0:whole * P, :].rearrange("(t p) d -> p t d", p=P),
                                 xv[:, 0:whole, :]).then_inc(s_out, 16)
                    sp.dma_start(out[whole * P:N_NODES, :], xv[0:rest, whole, :]).then_inc(s_out, 16)
                    sp.wait_ge(s_out, 32)
        for s in live:
            s.end()

    s_out, s_w3, s_held = sem("result_stored"), sem("weights3_in"), sem("waits_held")

    def counts(kind, names):
        return {n: Count(sem(f"{kind}_{n}")) for n in names}

    NAMES = (*(f"{n}{q}" for n in ("idx_in", "win_in", "rows_moved") for q in range(SLOTS)),
             "pick_ready", "sum_ready", "pre_ready", "z_ready", "msg_ready", "seg_ready", "acc_done", "deg_done",
             "tanh_ready", "max_ready", "maxT_ready", "max1_ready", "maxb_ready",
             "nmax_ready", "prob_ready", "comb_ready", "comb_out", "equal_ready", "index_ready", "masked", "merge",
             "vector_steps")
    in_order, windowed = counts("o", NAMES), counts("w", NAMES)

    def edge_pass(layer, c, window):
        hid = {0: HID, 1: D, 2: D, 3: HID}[layer]
        feat = layer in (0, 3)
        depth = WIN + (D_EDGE if feat else 0)
        loads = 3 if feat or layer == 1 else 2
        loads += layer == 1
        softmax = layer == 3
        table_q = h_tab if layer == 1 else q_tab[layer]
        per = dict.fromkeys(NAMES, GROUPS)
        for q in range(SLOTS):
            per[f"idx_in{q}"], per[f"win_in{q}"] = 16 * ITERS, 16 * loads * ITERS
            per[f"rows_moved{q}"] = 16 * SUB * ITERS
        per["vector_steps"] = {0: 0, 1: 4 * GROUPS, 2: 0, 3: 6 * GROUPS + 2}[layer]
        per["merge"] = 3
        live = {f"{n}{q}" for n in ("idx_in", "win_in", "rows_moved") for q in range(SLOTS)}
        live |= {"pick_ready", "pre_ready", "z_ready", "msg_ready", "vector_steps"}
        if layer == 1:
            live |= {"comb_ready", "comb_out", "equal_ready", "index_ready"}
            if window is not None:
                live |= {"masked"}
                per["vector_steps"] += 3 * GROUPS
        else:
            live |= {"sum_ready", "seg_ready", "acc_done"}
        if layer == 0:
            live |= {"deg_done"}
        if softmax:
            live |= {"tanh_ready", "max_ready", "maxT_ready", "max1_ready", "maxb_ready", "nmax_ready",
                     "prob_ready", "merge"}
        for n, count in c.items():
            count.begin(per[n] if n in live else 0, window)

        def run(eng, stages, link=None):
            last = -(-max(b for b, _ in stages) // SLOTS)

            def iteration(i):
                for r in range(SLOTS):
                    for behind, stage in stages:
                        q, ii = (r - behind) % SLOTS, i + (r - behind) // SLOTS
                        if not isinstance(i, int) or 0 <= ii < ITERS:
                            stage(q, ii)

            lead = LEAD if last else 1
            for i in range(lead):
                before = link.n if link else 0
                iteration(i)
            with eng.Fori(lead, ITERS) as i:
                if link:
                    link.enter(i, lead, link.n - before)
                iteration(i)
            if link:
                link.leave(ITERS - lead)
            for i in range(ITERS, ITERS + last):
                iteration(i)

        def g(q, i):
            return i * SLOTS + q + 1

        def sub(tile, j, width):
            return tile[:, j * width:(j + 1) * width]

        def as3(tile, width, stride=None):
            return tile[:, 0:SUB * (stride or width)].rearrange("p (j h) -> p j h", h=stride or width)[:, :, 0:width]

        def z3(q):
            return as3(z[q], hid)

        def m3(q, a=0, b=hid):
            return msg[q][:, :].rearrange("p (j h) -> p j h", h=HID + 1)[:, :, a:b]

        with nc.Block() as block:
            @block.sync
            def _(sp):
                def load(q, i):
                    n = i * SLOTS + q
                    if layer == 1:
                        c["index_ready"].wait(sp, g(q, i) - SLOTS)
                    else:
                        c[f"rows_moved{q}"].wait(sp, 16 * SUB * i)
                    sp.dma_start(idx[q][:, :], t["src_tiles"][:, bass.ds(n, 1), :].rearrange("p g j -> p (g j)"))\
                        .then_inc(c[f"idx_in{q}"].sem, 16)
                    base = sp.value_load(base_row[0:1, bass.ds(n, 1)], min_val=0, max_val=NPAD - WIN)
                    c["pre_ready"].wait(sp, g(q, i) - SLOTS)
                    s = c[f"win_in{q}"].sem
                    sp.dma_start(dst_b[q], t["dst_cols"][bass.ds(n, 1), :].to_broadcast((WIN, GE)))\
                        .then_inc(s, 16)
                    sp.dma_start(rows[q][0:WIN, 0:hid], table_q[bass.ds(base, WIN), :]).then_inc(s, 16)
                    if feat:
                        sp.dma_start(stack[q][WIN:depth, :],
                                     t["feat_cols"][bass.ds(n, 1), :, :].rearrange("g k e -> (g k) e"))\
                            .then_inc(s, 16)
                    if layer == 1:
                        c["msg_ready"].wait(sp, g(q, i) - SLOTS)
                        c["equal_ready"].wait(sp, g(q, i) - SLOTS)
                        sp.dma_start(z[q][:, 0:SUB * D],
                                     t["edge64"][bass.ds(n, 1), :, :].rearrange("g p e -> (g p) e"))\
                            .then_inc(s, 16)
                        sp.dma_start(src_b[q], t["src_cols"][bass.ds(n, 1), :].to_broadcast((P, GE)))\
                            .then_inc(s, 16)

                run(sp, [(0, load)])

            @block.gpsimd
            def _(pool):
                def gather(q, i):
                    c[f"idx_in{q}"].wait(pool, 16 * (i + 1))
                    c["msg_ready"].wait(pool, g(q, i) - SLOTS)
                    hold(pool)
                    for j in range(SUB):
                        pool.indirect_dma_start(
                            z[q][:, j * hid:(j + 1) * hid], None, p_tab[layer],
                            bass.IndirectOffsetOnAxis(ap=idx[q][:, j:j + 1], axis=0))\
                            .then_inc(c[f"rows_moved{q}"].sem, 16)

                def scatter(q, i):
                    c["index_ready"].wait(pool, g(q, i))
                    c["comb_out"].wait(pool, g(q, i))
                    before = (q - 2) % SLOTS
                    c[f"rows_moved{before}"].wait(pool, 16 * SUB * (i + (q >= 2)))
                    hold(pool)
                    for j in range(SUB):
                        pool.indirect_dma_start(
                            sums[q % 2 * SUB + j],
                            bass.IndirectOffsetOnAxis(ap=idx_e[q][:, j:j + 1], axis=0),
                            comb[q][:, j * D:(j + 1) * D], None, compute_op=ALU.add)\
                            .then_inc(c[f"rows_moved{q}"].sem, 16)

                run(pool, [(0, scatter if layer == 1 else gather)])
                for q in range(SLOTS):
                    c[f"rows_moved{q}"].wait(pool, 16 * SUB * ITERS)

            @block.tensor
            def _(pe):
                def pre(q, i):
                    c["pick_ready"].wait(pe, g(q, i))
                    c[f"win_in{q}"].wait(pe, 16 * loads * (i + 1))
                    c["z_ready"].wait(pe, g(q, i) - 2)
                    for j in range(SUB):
                        mm = nc.tensor.matmul(bank[q % 2][:, j * hid:(j + 1) * hid],
                                              stack[q][0:depth, j * P:(j + 1) * P], rows[q][0:depth, 0:hid],
                                              start=True, stop=True)
                    mm.then_inc(c["pre_ready"].sem, 1)

                def seg(q, i):
                    c["sum_ready"].wait(pe, g(q, i))
                    c["msg_ready"].wait(pe, g(q, i))
                    c["acc_done"].wait(pe, g(q, i) - 2)
                    if layer == 0:
                        c["deg_done"].wait(pe, g(q, i) - 2)
                    lo, hi = (D, HID + 1) if softmax else (0, hid)
                    for j in range(SUB):
                        mm = nc.tensor.matmul(bank[2 + q % 2][0:hi - lo, 0:WIN],
                                              msg[q][:, j * (HID + 1) + lo:j * (HID + 1) + hi],
                                              sub(onehot[q], j, WIN), start=j == 0, stop=j == SUB - 1)
                    if layer == 0:
                        for j in range(SUB):
                            mm = nc.tensor.matmul(bank[4 + q % 2][0:1, 0:WIN], ones_c[:, :],
                                                  sub(onehot[q], j, WIN), start=j == 0, stop=j == SUB - 1)
                    mm.then_inc(c["seg_ready"].sem, 1)

                def max_across(q, i):
                    c["max_ready"].wait(pe, g(q, i))
                    c["max1_ready"].wait(pe, g(q, i) - 2)
                    nc.tensor.transpose(bank[4 + q % 2][0:1, 0:P], gmax[q % 2][:, :], ident[:, :])\
                        .then_inc(c["maxT_ready"].sem, 1)

                def max_spread(q, i):
                    c["max1_ready"].wait(pe, g(q, i))
                    c["nmax_ready"].wait(pe, g(q, i) - 2)
                    nc.tensor.matmul(bank[6 + q % 2][:, 0:1], ones_r[0:1, :], gmax1[q % 2][:, :],
                                     start=True, stop=True).then_inc(c["maxb_ready"].sem, 1)

                def combine(q, i):
                    c["equal_ready"].wait(pe, g(q, i))
                    c["msg_ready" if window is None else "masked"].wait(pe, g(q, i))
                    c["comb_out"].wait(pe, g(q, i) - 2)
                    for j in range(SUB):
                        mm = nc.tensor.matmul(bank[2 + q % 2][:, j * D:(j + 1) * D], sub(equal[q % 2], j, P),
                                              m3(q)[:, j, :], start=True, stop=True)
                    mm.then_inc(c["comb_ready"].sem, 1)

                if layer == 1:
                    run(pe, [(0, pre), (2, combine)])
                elif softmax:
                    run(pe, [(5, seg), (3, max_spread), (2, max_across), (0, pre)])
                    c["merge"].wait(pe, 2)
                    nc.tensor.matmul(bank[7][0:D + 1, 0:GROUPS], ones_r[0:1, 0:D + 1], scale_row[:, :],
                                     start=True, stop=True).then_inc(c["merge"].sem, 1)
                else:
                    run(pe, [(0, pre), (2, seg)])

            @block.scalar
            def _(act):
                def relu(q, i):
                    c["z_ready"].wait(act, g(q, i))
                    if layer == 1:
                        c["comb_ready"].wait(act, g(q, i) - SLOTS)
                    else:
                        c["seg_ready"].wait(act, g(q, i) - SLOTS)
                    nc.scalar.activation(m3(q), z3(q), ACT.Relu).then_inc(c["msg_ready"].sem, 1)

                def tanh(q, i):
                    c["z_ready"].wait(act, g(q, i))
                    c["msg_ready"].wait(act, g(q, i) - 2)
                    nc.scalar.activation(half[q % 2][:, :], z[q][:, :], ACT.Tanh, scale=0.5)\
                        .then_inc(c["tanh_ready"].sem, 1)

                def exp(q, i):
                    c["nmax_ready"].wait(act, g(q, i))
                    c["sum_ready"].wait(act, g(q, i) - 2)
                    nc.scalar.activation(prob[q % 2][:, :], logit[q % 2][:, :], ACT.Exp, bias=nmax[q % 2][:, 0:1])\
                        .then_inc(c["prob_ready"].sem, 1)

                def combined(q, i):
                    c["comb_ready"].wait(act, g(q, i))
                    c[f"rows_moved{q}"].wait(act, 16 * SUB * i)
                    nc.scalar.activation(comb[q], bank[2 + q % 2][:, 0:SUB * D], ACT.Copy)\
                        .then_inc(c["comb_out"].sem, 1)

                if layer == 1:
                    run(act, [(1, relu), (2, combined)])
                elif softmax:
                    run(act, [(4, exp), (1, tanh)])
                    c["merge"].wait(act, 1)
                    nc.scalar.activation(scale_row[:, :], gmax_row[:, :], ACT.Exp, bias=gm1[:, 1:2])\
                        .then_inc(c["merge"].sem, 1)
                else:
                    run(act, [(1, relu)])

            @block.vector
            def _(dve):
                link = Link(dve, c["vector_steps"])

                def pick(q, i):
                    c[f"win_in{q}"].wait(dve, 16 * loads * (i + 1))
                    nc.vector.tensor_scalar(stack[q][0:WIN, :], dst_b[q],
                                            base_col[:, bass.ds(i * SLOTS + q, 1)], None,
                                            ALU.is_equal).then_inc(c["pick_ready"].sem, 1)

                def window_onehot(q, i):
                    c["seg_ready"].wait(dve, g(q, i) - SLOTS)
                    return nc.vector.tensor_tensor(
                        onehot[q][:, :].rearrange("p (j w) -> p j w", w=WIN),
                        dst_rel[:, bass.ds((i * SLOTS + q) * SUB, SUB)][:, :, None].to_broadcast((P, SUB, WIN)),
                        iota_w[:, None, :].to_broadcast((P, SUB, WIN)), ALU.is_equal)

                def plain_onehot(q, i):
                    window_onehot(q, i).then_inc(c["sum_ready"].sem, 1)

                def add(q, i):
                    c["pre_ready"].wait(dve, g(q, i))
                    if layer != 1:
                        c[f"rows_moved{q}"].wait(dve, 16 * SUB * (i + 1))
                    nc.vector.tensor_tensor(z[q][:, 0:SUB * hid], z[q][:, 0:SUB * hid],
                                            bank[q % 2][:, 0:SUB * hid], ALU.add).then_inc(c["z_ready"].sem, 1)

                def accumulate(q, i):
                    hold(dve)
                    base = dve.value_load(base_row[0:1, bass.ds(i * SLOTS + q, 1)], min_val=0, max_val=NPAD - WIN)
                    at = bass.ds(base, WIN)
                    c["seg_ready"].wait(dve, g(q, i))
                    c["acc_done"].wait(dve, g(q, i) - 1)
                    nc.vector.tensor_tensor(acc[0:hid, at], acc[0:hid, at], bank[2 + q % 2][0:hid, 0:WIN],
                                            ALU.add).then_inc(c["acc_done"].sem, 1)
                    if layer == 0:
                        c["deg_done"].wait(dve, g(q, i) - 1)
                        nc.vector.tensor_tensor(deg[:, at], deg[:, at], bank[4 + q % 2][0:1, 0:WIN],
                                                ALU.add).then_inc(c["deg_done"].sem, 1)

                def silu(q, i):
                    c["tanh_ready"].wait(dve, g(q, i))
                    c["seg_ready"].wait(dve, g(q, i) - SLOTS)
                    nc.vector.scalar_tensor_tensor(m3(q), half[q % 2][:, :].rearrange("p (j h) -> p j h", h=HID), 1.0,
                                                   z3(q), ALU.add, ALU.mult).then_inc(c["msg_ready"].sem, 1)
                    c["msg_ready"].wait(dve, g(q, i))
                    p3 = prod[:, 0:SUB * D].rearrange("p (j h) -> p j h", h=D)
                    link(nc.vector.tensor_tensor(p3, m3(q, 0, D), wa2[:, None, :].to_broadcast((P, SUB, D)),
                                                 ALU.mult))
                    c["prob_ready"].wait(dve, g(q, i) - 2)
                    link(nc.vector.tensor_reduce(logit[q % 2][:, :], p3, AX.X, ALU.add))
                    link(nc.vector.tensor_scalar(logit[q % 2][:, :], logit[q % 2][:, :], ba2[:, 0:1], None, ALU.add))
                    c["maxT_ready"].wait(dve, g(q, i) - 2)
                    nc.vector.tensor_reduce(gmax[q % 2][:, :], logit[q % 2][:, :], AX.X,
                                            ALU.max).then_inc(c["max_ready"].sem, 1)

                def group_max(q, i):
                    c["maxT_ready"].wait(dve, g(q, i))
                    c["maxb_ready"].wait(dve, g(q, i) - 2)
                    nc.vector.tensor_reduce(gmax1[q % 2][:, :], bank[4 + q % 2][0:1, 0:P], AX.X,
                                            ALU.max).then_inc(c["max1_ready"].sem, 1)
                    c["max1_ready"].wait(dve, g(q, i))
                    link(nc.vector.tensor_copy(gmax_row[:, bass.ds(i * SLOTS + q, 1)], gmax1[q % 2][:, :]))

                def negate_max(q, i):
                    c["maxb_ready"].wait(dve, g(q, i))
                    c["prob_ready"].wait(dve, g(q, i) - 2)
                    nc.vector.tensor_scalar(nmax[q % 2][:, :], bank[6 + q % 2][:, 0:1], -1.0, None,
                                            ALU.mult).then_inc(c["nmax_ready"].sem, 1)

                def weigh(q, i):
                    link(window_onehot(q, i))
                    c["prob_ready"].wait(dve, g(q, i))
                    o3 = onehot[q][:, :].rearrange("p (j w) -> p j w", w=WIN)
                    nc.vector.tensor_tensor(o3, o3, prob[q % 2][:, :, None].to_broadcast((P, SUB, WIN)),
                                            ALU.mult).then_inc(c["sum_ready"].sem, 1)

                def keep(q, i):
                    c["seg_ready"].wait(dve, g(q, i))
                    nc.vector.tensor_copy(parts[:, bass.ds((i * SLOTS + q) * WIN, WIN)],
                                          bank[2 + q % 2][0:D + 1, 0:WIN]).then_inc(c["acc_done"].sem, 1)

                def same(q, i):
                    c[f"idx_in{q}"].wait(dve, 16 * (i + 1))
                    c["comb_ready"].wait(dve, g(q, i) - 2)
                    e3 = equal[q % 2].rearrange("p (j e) -> p j e", e=P)
                    d3 = prod[:, :].rearrange("p (j e) -> p j e", e=P)
                    nc.vector.tensor_tensor(e3, src_b[q].rearrange("p (j e) -> p j e", e=P),
                                            idx[q][:, :, None].to_broadcast((P, SUB, P)),
                                            ALU.is_equal).then_inc(c["equal_ready"].sem, 1)
                    c["equal_ready"].wait(dve, g(q, i))
                    link(nc.vector.tensor_tensor(d3, e3, earlier[:, None, :].to_broadcast((P, SUB, P)), ALU.mult))
                    link(nc.vector.tensor_reduce(dup[:, 0:SUB], d3, AX.X, ALU.max))
                    link(nc.vector.tensor_scalar(dup[:, SUB:2 * SUB], idx[q][:, :], dummy[:, 0:1], None,
                                                 ALU.subtract))
                    link(nc.vector.tensor_tensor(dup[:, SUB:2 * SUB], dup[:, SUB:2 * SUB], dup[:, 0:SUB], ALU.mult))
                    c[f"rows_moved{q}"].wait(dve, 16 * SUB * i)
                    nc.vector.tensor_tensor(idx_e[q][:, :], idx[q][:, :], dup[:, SUB:2 * SUB],
                                            ALU.subtract).then_inc(c["index_ready"].sem, 1)

                def mask(q, i):
                    rel = dst_rel[:, bass.ds((i * SLOTS + q) * SUB, SUB)]
                    link(nc.vector.tensor_scalar(dup[:, 2 * SUB:3 * SUB], rel, 0.0, None, ALU.is_ge))
                    link(nc.vector.tensor_scalar(dup[:, 3 * SUB:4 * SUB], rel, float(WIN), None, ALU.is_lt))
                    link(nc.vector.tensor_tensor(dup[:, 2 * SUB:3 * SUB], dup[:, 2 * SUB:3 * SUB],
                                                 dup[:, 3 * SUB:4 * SUB], ALU.mult))
                    c["msg_ready"].wait(dve, g(q, i))
                    nc.vector.tensor_tensor(m3(q), m3(q),
                                            dup[:, 2 * SUB:3 * SUB][:, :, None].to_broadcast((P, SUB, D)),
                                            ALU.mult).then_inc(c["masked"].sem, 1)

                if layer == 1:
                    run(dve, [(0, pick), (1, add), (1, same)] + [(1, mask)] * (window is not None), link)
                elif softmax:
                    run(dve, [(6, keep), (5, weigh), (4, negate_max), (3, group_max), (2, silu), (1, add), (0, pick)],
                        link)
                    link(nc.vector.tensor_reduce(gm1[:, 0:1], gmax_row[:, :], AX.X, ALU.max))
                    nc.vector.tensor_scalar(gm1[:, 1:2], gm1[:, 0:1], -1.0, None, ALU.mult)\
                        .then_inc(c["merge"].sem, 1)
                    c["merge"].wait(dve, 3)
                    c["acc_done"].wait(dve, GROUPS)
                    v = parts[:, :].rearrange("p (g w) -> p g w", w=WIN)
                    link(nc.vector.tensor_tensor(
                        v, v, bank[7][0:D + 1, 0:GROUPS][:, :, None].to_broadcast((D + 1, GROUPS, WIN)), ALU.mult))

                    def merge(i):
                        for q in range(SLOTS):
                            n = i * SLOTS + q
                            hold(dve)
                            base = dve.value_load(base_row[0:1, bass.ds(n, 1)], min_val=0, max_val=NPAD - WIN)
                            at = bass.ds(base, WIN)
                            link(nc.vector.tensor_tensor(acc[0:D + 1, at], acc[0:D + 1, at],
                                                         parts[:, bass.ds(n * WIN, WIN)], ALU.add))

                    link.loop(dve, merge, hold)
                else:
                    run(dve, [(0, pick), (0, plain_onehot), (1, add), (3, accumulate)], link)
                assert link.n == per["vector_steps"], (layer, link.n, per["vector_steps"])
        for count in c.values():
            count.end(1 if window is None else WINDOWS)

    def next_window():
        with nc.Block() as block:
            @block.vector
            def _(dve):
                n = [0]

                def link(ins):
                    n[0] += 1
                    ins.then_inc(s_next, 1)
                    dve.wait_ge(s_next, n[0])

                dve.sem_clear(s_next)
                link(nc.vector.tensor_scalar(win_id[:, :], win_id[:, :], float(WIN), None, ALU.add))
                link(nc.vector.tensor_tensor(dup[:, 0:1], win_id[:, :], place[:, :], ALU.add))
                nc.vector.tensor_copy(base_row[:, :], win_id[0:1, 0:1].to_broadcast((1, GROUPS)))
                nc.vector.tensor_copy(base_col, dup[DST_AT:DST_AT + WIN, 0:1].to_broadcast((WIN, GROUPS)))
                link(nc.vector.tensor_scalar(dst_rel[:, :], dst_i[:, :], win_id[:, 0:1], None, ALU.subtract))

    def first_window():
        with nc.Block() as block:
            @block.vector
            def _(dve):
                nc.vector.memset(win_id[:, :], -float(WIN))

    s_next = sem("next_window")

    def edge_phase(layer):
        with nc.If(widest < WIN):
            edge_pass(layer, in_order, None)
        with nc.Else():
            first_window()
            with nc.Fori(0, WINDOWS) as w:
                next_window()
                edge_pass(layer, windowed, w)

    node_phase(None, 0)
    for layer in range(4):
        edge_phase(layer)
        node_phase(layer, layer + 1 if layer < 3 else None)


def kernel(**inputs):
    import numpy as np
    import concourse.bacc as bacc
    from concourse.bass_utils import run_bass_kernel_spmd

    nc = bacc.Bacc("TRN2", target_bir_lowering=False, num_devices=1)
    a = {k: np.ascontiguousarray(v) for k, v in inputs.items()}

    def padded(v, fill):
        out = np.full((GROUPS * GE, *v.shape[1:]), fill, v.dtype)
        out[:N_EDGES] = v
        return out

    src, dst = (padded(a.pop(k), N_NODES) for k in ("src", "dst"))
    feat = padded(a.pop("edge_attr_32"), 0).reshape(GROUPS, P, SUB, D_EDGE)
    a["edge64"] = padded(a.pop("edge_attr_64"), 0).reshape(GROUPS, P, SUB * D)
    a["feat_cols"] = np.ascontiguousarray(feat.transpose(0, 3, 2, 1)).reshape(GROUPS, D_EDGE, GE)
    a["dst_groups"] = dst.reshape(GROUPS, GE)
    for name, v in (("src", src), ("dst", dst)):
        v = v.reshape(GROUPS, P, SUB)
        a[name + "_tiles"] = np.ascontiguousarray(v.transpose(1, 0, 2))
        a[name + "_cols"] = np.ascontiguousarray(v.transpose(0, 2, 1)).reshape(GROUPS, GE)
    t = {k: nc.dram_tensor("in_" + k, v.shape, mybir.dt.from_np(v.dtype), kind="ExternalInput").ap()
         for k, v in a.items()}
    out = nc.dram_tensor("out", (N_NODES, D), F32, kind="ExternalOutput").ap()
    gnn(nc, t, out)
    r = run_bass_kernel_spmd(nc, [{"in_" + k: v for k, v in a.items()}], core_ids=[0])
    return r.results[0]["out"]
```

```python
import concourse.bass as bass
from concourse import mybir
from contextlib import ExitStack

F32 = mybir.dt.float32
I32 = mybir.dt.int32
ALU = mybir.AluOpType
ACT = mybir.ActivationFunctionType
AX = mybir.AxisListType

N_NODES, D, D_EDGE, HID = 6250, 64, 32, 128
N_EDGES = 200000
LN_EPS = 1e-5
FAR = 1e30
P = 128
SUB = 4
GE = SUB * P
SLOTS = 4
GROUPS = -(-N_EDGES // (GE * SLOTS)) * SLOTS
ITERS = GROUPS // SLOTS
TILES = -(-N_NODES // P)
NPAD = TILES * P
WIN = 32
WINDOWS = NPAD // WIN
CT = 7
CHUNKS = TILES // CT
CN = CT * P
HALF = CN // 2
MERGED = next(n for n in (28, 14, 8, 6, 4) if GROUPS % n == 0)
TABLES = 2 * SUB
LEAD = 3
GPC = GROUPS // 4
assert TABLES * CT * D <= (SLOTS + 3) * SUB * HID
assert GROUPS * WIN >= NPAD and SLOTS * SUB * (HID + 1) >= CT * 2 * HID and WIN + D_EDGE >= D
DST_AT = WIN + D_EDGE
SUM_ROW = (NPAD + P) * D // P // 5
assert 3 * CT * D + CT * HID + CN <= NPAD
assert GROUPS - N_EDGES // GE <= 2
assert TILES % CT == 0 and GROUPS % 4 == 0 and NPAD % WIN == 0 and NPAD > N_NODES


class Count:

    def __init__(self, sem):
        self.sem, self.base, self.per_pass, self.window = sem, 0, 0, None

    def begin(self, per_pass, window):
        self.per_pass, self.window = per_pass, window

    def end(self, passes):
        self.base += self.per_pass * passes

    def wait(self, eng, n):
        if isinstance(n, int) and n <= 0:
            return
        value = n + self.base
        if self.window is not None:
            value = self.window * self.per_pass + value
        eng.wait_ge(self.sem, value)


class Link:

    def __init__(self, eng, count):
        self.eng, self.count, self.n, self.inside = eng, count, 0, None

    def __call__(self, ins):
        self.n += 1
        ins.then_inc(self.count.sem, 1)
        if self.inside is None:
            self.count.wait(self.eng, self.n)
        else:
            i, first, each = self.inside
            self.count.wait(self.eng, (i - first) * each + self.n)

    def enter(self, i, first, each):
        self.inside, self.start = (i, first, each), self.n

    def leave(self, iterations):
        _, _, each = self.inside
        assert self.n - self.start == each, (self.n, self.start, each)
        self.inside, self.n = None, self.start + each * iterations


def gnn(nc, t, out):
    ctx = ExitStack()
    with ctx:
        _gnn(nc, t, out, ctx)


def _gnn(nc, t, out, ctx):
    def sb(name, shape, dt=F32):
        return ctx.enter_context(nc.sbuf_tensor(name, shape, dt))

    def sem(name):
        return ctx.enter_context(nc.semaphore(name))

    def dram(name, shape, dt=F32):
        return nc.dram_tensor(name, shape, dt, kind="Internal").ap()

    x_all = sb("x_all", [P, TILES * D])
    work = sb("work", [P, TILES * D + (SLOTS + 3) * SUB * HID])
    h_all = work[:, 0:TILES * D]
    scratch = work[:, TILES * D:]
    acc2 = work[0:D + 1, 0:NPAD]
    hT = sb("hT", [D + 2, NPAD])
    acc = sb("acc", [P, NPAD])
    parts = sb("parts", [D + 1, GROUPS * WIN])
    deg = parts[0:1, 0:NPAD]
    dst_i = sb("dst_i", [P, GROUPS * SUB], I32)
    dst_rel = sb("dst_rel", [P, GROUPS * SUB])
    base_row = sb("base_row", [1, GROUPS], I32)
    base_cols = sb("base_col", [DST_AT + WIN, GROUPS])
    base_col = base_cols[DST_AT:DST_AT + WIN, :]
    win_id = sb("win_id", [P, 1])
    ident = sb("ident", [P, P])
    earlier = sb("earlier", [P, P])
    iota_w = sb("iota_w", [P, WIN])
    place = sb("place", [P, 1])
    dummy = sb("dummy_row", [P, 1])
    ones_c = sb("ones_c", [P, 1])
    ones_r = sb("ones_r", [P, P])
    eps_c = sb("eps_c", [P, 1])
    idx = [sb(f"idx{q}", [P, SUB], I32) for q in range(SLOTS)]
    stack_all = sb("stack_all", [DST_AT + WIN, SLOTS * GE])
    dst_b = [stack_all[DST_AT:DST_AT + WIN, q * GE:(q + 1) * GE] for q in range(SLOTS)]
    stack = [stack_all[:, q * GE:(q + 1) * GE] for q in range(SLOTS)]
    rows = [sb(f"rows{q}", [WIN + D_EDGE, HID]) for q in range(SLOTS)]
    onehot = [sb(f"onehot{q}", [P, SUB * WIN]) for q in range(SLOTS)]
    z = [scratch[:, q * SUB * HID:(q + 1) * SUB * HID] for q in range(SLOTS)]
    msg_all = sb("msg_all", [P, SLOTS * SUB * (HID + 1)])
    msg = [msg_all[:, q * SUB * (HID + 1):(q + 1) * SUB * (HID + 1)] for q in range(SLOTS)]
    half = [scratch[:, (SLOTS + b) * SUB * HID:(SLOTS + b + 1) * SUB * HID] for b in range(2)]
    prod = scratch[:, (SLOTS + 2) * SUB * HID:]
    logit = [sb(f"logit{b}", [P, SUB]) for b in range(2)]
    gmax = [sb(f"gmax{b}", [P, 1]) for b in range(2)]
    gmax1 = [sb(f"gmax1{b}", [1, 1]) for b in range(2)]
    biased = [sb(f"biased{b}", [1, 1]) for b in range(2)]
    nmax = [sb(f"nmax{b}", [P, 1]) for b in range(2)]
    prob = [sb(f"prob{b}", [P, SUB]) for b in range(2)]
    gmax_row = sb("gmax_row", [1, GROUPS + 1])
    scale_row = sb("scale_row", [1, GROUPS + 1])
    tot = sb("tot", [D + 1, 2])
    itot = sb("itot", [D + 1, 1])
    gm1 = sb("gm1", [1, 2])
    dup = sb("dup", [P, 4 * SUB])
    equal = [half[b][:, :] for b in range(2)]
    src_b = [acc[:, q * GE:(q + 1) * GE].bitcast(I32) for q in range(SLOTS)]
    comb = [acc[:, SLOTS * GE + q * SUB * D:SLOTS * GE + (q + 1) * SUB * D] for q in range(SLOTS)]
    idx_e = [sb(f"idx_e{q}", [P, SUB], I32) for q in range(SLOTS)]
    hTc = sb("hTc", [D + 1, CN])
    mixed, own_h, total = (acc[:, k * CT * D:(k + 1) * CT * D] for k in range(3))
    sq1 = acc[:, 3 * CT * D:3 * CT * D + CT * HID]
    mixTc = acc[0:D + 1, 3 * CT * D + CT * HID:3 * CT * D + CT * HID + CN]
    st1 = sb("st1", [P, 3 * CT])
    u1T = sb("u1T", [HID, CN])
    pq = msg_all[:, 0:CT * 2 * HID]
    xm = sb("xm", [P, CT * HID])
    sq = sb("sq", [P, CT * D])
    st = sb("st", [P, 4 * CT])
    tabs = [scratch[:, k * CT * D:(k + 1) * CT * D] for k in range(TABLES)]
    zero_row = sb("zero_row", [P, SUM_ROW])
    w_pq = [sb(f"w_pq{l}", [D + 1, 2 * HID]) for l in (0, 2, 3)]
    w_pq = {0: w_pq[0], 2: w_pq[1], 3: w_pq[2]}
    w_agg = {l: sb(f"w_agg{l}", [HID if l == 0 else D + 1, D]) for l in (0, 2, 3)}
    b_agg = {l: sb(f"b_agg{l}", [D, 1]) for l in (0, 2, 3)}
    FOLDED = ((0, HID, HID, 0), (2, D, D, HID), (3, D + 1, D, HID + D))
    aggT = stack_all[0:D, 0:HID + D + D + 1]
    w_sum = {l: sb(f"w_sum{l}", [HID if l == 0 else D + 1, HID if l == 0 else D]) for l in (0, 2, 3)}
    b_sum = sb("b_sum", [1, HID + 2 * D])
    w_u1h = {l: sb(f"w_u1h{l}", [D + 2, HID]) for l in (0, 1, 2, 3)}
    w_u1a = {l: sb(f"w_u1a{l}", [D, HID]) for l in (0, 2, 3)}
    w_u2 = {l: sb(f"w_u2{l}", [HID, D]) for l in (0, 1, 2, 3)}
    b_u2 = {l: sb(f"b_u2{l}", [P, D]) for l in (0, 1, 2, 3)}
    ln_gb = sb("ln_gb", [P, 2])
    eps1 = sb("eps1", [P, 1])
    wa2 = sb("wa2", [P, D])
    ba2 = sb("ba2", [P, 1])
    bank = [ctx.enter_context(nc.psum_tensor(f"bank{i}", [P, 512], F32)) for i in range(8)]

    hid_of = {0: HID, 2: D, 3: HID}
    p_tab = {l: dram(f"p_tab{l}", (NPAD, hid_of[l])) for l in (0, 2, 3)}
    q_tab = {l: dram(f"q_tab{l}", (NPAD, hid_of[l])) for l in (0, 2, 3)}
    h_tab = dram("h_tab", (NPAD, D))
    sums = [dram(f"sums{k}", (NPAD + P, D)) for k in range(TABLES)]
    dst_f = dram("dst_f", (GROUPS, GE))
    base_d = dram("base_d", (GROUPS,), I32)
    span_d = dram("span_d", (GROUPS,), I32)

    s_const, s_w, s_dst, s_dc, s_bd, s_bb = (sem(n) for n in (
        "constants_made", "weights_in", "dst_in", "index_steps", "bases_out", "bases_in"))
    s_cast = sem("dst_cast")
    s_zero, s_zt = sem("zeroed"), sem("sums_zeroed")
    CONSTS = 13
    weights, biases = [], []
    for l, w1, b1 in ((0, "L0_gnn_mW1", "L0_gnn_mb1"), (2, "L2_gnn_ew1", "L2_gnn_eb1")):
        h = hid_of[l]
        weights += [(w_pq[l][0:D, 0:h], t[w1][0:D, :]), (w_pq[l][0:D, h:2 * h], t[w1][D:2 * D, :]),
                    (w_pq[l][D:D + 1, h:2 * h], t[b1][None, :])]
    for o, w1, b1 in ((0, "L3_gnn_Wa1", "L3_gnn_ba1"), (D, "L3_gnn_W1", "L3_gnn_b1")):
        weights += [(w_pq[3][0:D, o:o + D], t[w1][0:D, :]), (w_pq[3][0:D, HID + o:HID + o + D], t[w1][D:2 * D, :]),
                    (w_pq[3][D:D + 1, HID + o:HID + o + D], t[b1][None, :])]
    weights += [(w_agg[0][:, 0:D], t["L0_gnn_mW2"]), (w_agg[2][0:D, 0:D], t["L2_gnn_ew2"]),
                (w_agg[3][0:D, 0:D], t["L3_gnn_W2"]), (w_agg[3][D:D + 1, 0:D], t["L3_gnn_b2"][None, :]),
                (b_agg[0][:, :], t["L0_gnn_mb2"][:, None]), (b_agg[2][:, :], t["L2_gnn_eb2"][:, None]),
                (b_agg[3][:, :], t["L3_gnn_b2"][:, None])]
    for l, w1, b1, w2, b2 in ((0, "L0_gnn_uW1", "L0_gnn_ub1", "L0_gnn_uW2", "L0_gnn_ub2"),
                              (1, "L1_gnn_W1", "L1_gnn_b1", "L1_gnn_W2", "L1_gnn_b2"),
                              (2, "L2_gnn_vw1", "L2_gnn_vb1", "L2_gnn_vw2", "L2_gnn_vb2"),
                              (3, "L3_gnn_Wu1", "L3_gnn_bu1", "L3_gnn_Wu2", "L3_gnn_bu2")):
        h = t[w1].shape[1]
        biases += [(w_u1h[l][D:D + 1, 0:h], t[b1][None, :])]
        weights += [(w_u1h[l][0:D, 0:h], t[w1][0:D, :]),
                    (w_u2[l][0:h, :], t[w2]), (b_u2[l][:, :], t[b2][None, :].to_broadcast((P, D)))]
        if l != 1:
            weights += [(w_u1a[l][:, 0:h], t[w1][D:2 * D, :])]
    weights += [(ln_gb[:, 0:1], t["L1_gnn_ln_g"][:, None]),
                (ln_gb[:, 1:2], t["L1_gnn_ln_b"][:, None]),
                (eps1[:, :], t["L1_gnn_eps"][None, :].to_broadcast((P, 1))),
                (wa2[:, :], t["L3_gnn_Wa2"].rearrange("d a -> a d").to_broadcast((P, D))),
                (ba2[:, :], t["L3_gnn_ba2"][None, :].to_broadcast((P, 1)))]
    for q in range(SLOTS):
        weights += [(rows[q][WIN:WIN + D_EDGE, 0:HID], t["L0_gnn_mW1"][2 * D:2 * D + D_EDGE, :])]
    WEIGHTS = len(weights) + len(biases) + 2
    whole = N_NODES // P
    rest = N_NODES - whole * P
    base_b = half[0][:, 0:GROUPS].bitcast(I32)
    gcols = [zz[0:GPC, :].bitcast(I32) for zz in z]
    bmin, bmax = st[0:GPC, 0:4], st[0:GPC, 4:8]
    bint = idx_e[0][0:GPC, :]
    sint = idx_e[1][0:GPC, :]

    with nc.Block() as block:
        @block.gpsimd
        def _(pool):
            nc.gpsimd.memset(ident[:, :], 0.0).then_inc(s_const, 1)
            nc.gpsimd.memset(earlier[:, :], 1.0).then_inc(s_const, 1)
            pool.wait_ge(s_const, 2)
            nc.gpsimd.affine_select(out=ident[:, :], in_=ident[:, :], compare_op=ALU.not_equal, fill=1.0,
                                    base=0, pattern=[[-1, P]], channel_multiplier=1).then_inc(s_const, 1)
            nc.gpsimd.affine_select(out=earlier[:, :], in_=earlier[:, :], compare_op=ALU.is_gt, fill=0.0,
                                    base=0, pattern=[[-1, P]], channel_multiplier=1).then_inc(s_const, 1)
            nc.gpsimd.iota(iota_w[:, :], pattern=[[1, WIN]], base=0, channel_multiplier=0,
                           allow_small_or_imprecise_dtypes=True).then_inc(s_const, 1)
            nc.gpsimd.iota(place[:, :], pattern=[[1, 1]], base=-DST_AT, channel_multiplier=1,
                           allow_small_or_imprecise_dtypes=True).then_inc(s_const, 1)
            nc.gpsimd.iota(dummy[:, :], pattern=[[1, 1]], base=NPAD, channel_multiplier=1,
                           allow_small_or_imprecise_dtypes=True).then_inc(s_const, 1)
            for tile, value in ((ones_c, 1.0), (ones_r, 1.0), (eps_c, LN_EPS), (acc, 0.0), (zero_row, 0.0), (deg, 0.0)):
                nc.gpsimd.memset(tile[:, :], value).then_inc(s_const, 1)
            pool.wait_ge(s_const, CONSTS)
            rows_of = lambda a: a.rearrange("g e -> (g e)").rearrange("(p n) -> p n", p=P)
            pool.dma_start(rows_of(dst_f), rows_of(t["dst_cols"])).then_inc(s_cast, 16)
            nc.gpsimd.memset(hT[D:D + 2, :], 1.0).then_inc(s_const, 1)
            pool.wait_ge(s_cast, 16)
            pool.wait_ge(s_const, CONSTS + 1)

        @block.sync
        def _(sp):
            for c in range(4):
                sp.dma_start(gcols[c], t["dst_groups"].rearrange("(p c) e -> c p e", c=4)[c]).then_inc(s_dst, 16)
            sp.dma_start(dst_i[:, :].rearrange("p (g j) -> p g j", j=SUB),
                         t["dst_tiles"]).then_inc(s_dst, 16)
            sp.wait_ge(s_dc, 11)
            sp.dma_start(base_d.rearrange("(p c) -> p c", c=4), bint).then_inc(s_bd, 16)
            sp.dma_start(span_d.rearrange("(p c) -> p c", c=4), sint).then_inc(s_bd, 16)
            sp.wait_ge(s_bd, 32)
            sp.dma_start(base_row[:, :], base_d[None, :]).then_inc(s_bb, 16)
            sp.dma_start(gmax_row[:, 0:GROUPS].bitcast(I32), span_d[None, :]).then_inc(s_bb, 16)
            sp.dma_start(base_b, base_d[None, :].to_broadcast((P, GROUPS))).then_inc(s_bb, 16)
            sp.wait_ge(s_bb, 48)

        @block.scalar
        def _(act):
            xv = x_all[:, :].rearrange("p (t d) -> p t d", d=D)
            act.dma_start(xv[:, 0:whole, :],
                          t["x"][0:whole * P, :].rearrange("(t p) d -> p t d", p=P)).then_inc(s_w, 16)
            with nc.allow_non_contiguous_dma(reason="a column of weights"):
                for to, of in weights:
                    act.dma_start(to, of).then_inc(s_w, 16)
            act.wait_ge(s_zero, 10)
            for to, of in biases:
                act.dma_start(to, of).then_inc(s_w, 16)
            act.dma_start(xv[0:rest, whole, :], t["x"][whole * P:N_NODES, :]).then_inc(s_w, 16)
            act.wait_ge(s_w, 16 * WEIGHTS)

        @block.vector
        def _(dve):
            nc.vector.memset(x_all[:, whole * D:], 0.0).then_inc(s_zero, 1)
            nc.vector.memset(gmax_row[:, GROUPS:], -FAR).then_inc(s_zero, 1)
            nc.vector.memset(hTc[D:D + 1, :], 1.0).then_inc(s_zero, 1)
            for l in (0, 2, 3):
                nc.vector.memset(w_u1h[l][D:D + 2, :], 0.0).then_inc(s_zero, 1)
            nc.vector.memset(w_sum[2][D:D + 1, :], 0.0).then_inc(s_zero, 1)
            for l in (0, 2, 3):
                nc.vector.memset(w_pq[l][D:D + 1, 0:hid_of[l]], 0.0).then_inc(s_zero, 1)
            dve.wait_ge(s_dst, 80)
            for c in range(4):
                nc.vector.tensor_reduce(bmin[:, c:c + 1], gcols[c], AX.X, ALU.min).then_inc(s_dc, 1)
                nc.vector.tensor_reduce(bmax[:, c:c + 1], gcols[c], AX.X, ALU.max).then_inc(s_dc, 1)
            dve.wait_ge(s_dc, 8)
            nc.vector.tensor_scalar(bmin, bmin, float(NPAD - WIN), None, ALU.min).then_inc(s_dc, 1)
            dve.wait_ge(s_dc, 9)
            nc.vector.tensor_copy(bint, bmin).then_inc(s_dc, 1)
            nc.vector.tensor_tensor(sint, bmax, bmin, ALU.subtract).then_inc(s_dc, 1)
            dve.wait_ge(s_bb, 48)
            dve.wait_ge(s_const, CONSTS)
            nc.vector.tensor_scalar(base_col, base_b[DST_AT:DST_AT + WIN, :], place[DST_AT:DST_AT + WIN, 0:1], None,
                                    ALU.add).then_inc(s_dc, 1)
            nc.vector.tensor_tensor(dst_rel[:, :].rearrange("p (g j) -> p g j", j=SUB),
                                    dst_i[:, :].rearrange("p (g j) -> p g j", j=SUB),
                                    base_b[:, :, None].to_broadcast((P, GROUPS, SUB)),
                                    ALU.subtract).then_inc(s_dc, 1)
            nc.vector.tensor_reduce(gm1[:, 0:1], gmax_row[:, 0:GROUPS].bitcast(I32), AX.X, ALU.max).then_inc(s_dc, 1)
            dve.wait_ge(s_dc, 14)
            nc.vector.tensor_copy(gm1[:, 1:2].bitcast(I32), gm1[:, 0:1]).then_inc(s_dc, 1)
            dve.wait_ge(s_w, 16 * WEIGHTS)
            nc.vector.tensor_scalar(wa2[:, :], wa2[:, :], 0.5, None, ALU.mult).then_inc(s_dc, 1)
            nc.vector.tensor_scalar(w_agg[3][0:D, :], w_agg[3][0:D, :], 0.5, None, ALU.mult).then_inc(s_dc, 1)
            nc.vector.tensor_scalar(w_u2[3][0:D, :], w_u2[3][0:D, :], 0.5, None, ALU.mult).then_inc(s_dc, 1)
            nc.vector.memset(win_id[:, :], -float(WIN)).then_inc(s_dc, 1)
            nc.vector.tensor_scalar(eps1[:, :], eps1[:, :], 1.0, None, ALU.add).then_inc(s_dc, 1)
            nc.vector.tensor_reduce(st[0:D + 1, 0:1], w_u1h[1][0:D + 1, :], AX.X, ALU.add).then_inc(s_dc, 1)
            dve.wait_ge(s_dc, 21)
            nc.vector.tensor_scalar(st[0:D + 1, 1:2], st[0:D + 1, 0:1], 1.0 / HID, None, ALU.mult).then_inc(s_dc, 1)
            dve.wait_ge(s_dc, 22)
            nc.vector.tensor_scalar(w_u1h[1][0:D + 1, :], w_u1h[1][0:D + 1, :], st[0:D + 1, 1:2], None,
                                    ALU.subtract).then_inc(s_dc, 1)
            dve.wait_ge(s_dc, 23)

    widest = nc.values_load(gm1[0:1, 1:2].bitcast(I32), min_val=0, max_val=NPAD)

    def hold(eng):
        eng.sem_inc(s_held, 1)

    class Stage:

        def __init__(self, name, by=1):
            self.sem, self.by, self.base = sem(name), by, 0

        def wait(self, eng, i, before=0, left=0):
            if isinstance(i, int) and i < before:
                return
            eng.wait_ge(self.sem, (i - before + 1) * self.by + self.base - left)

        def end(self):
            self.base += self.by * CHUNKS

    hidden, hidden_tanh, hidden_out = (Stage(n, 2) for n in ("hidden", "hidden_tanh", "hidden_out"))
    y_done, x_new = Stage("y_done"), Stage("x_new")
    own, tab_sum, mix, mixT, mixT_out, h1, square1, var1, std1, h1n, h1T = (Stage(n) for n in (
        "own_part", "tab_sum", "mix", "mixT", "mixT_out", "h1", "square1", "var1", "std1", "h1n", "h1T"))
    tab_in = [Stage(f"tab_in{b}", 16 * TABLES // 2) for b in range(2)]
    tab_sum.by = 2
    var, std, h_ready, trans, trans_out, pq_ready, pq_out = (Stage(n) for n in (
        "var", "std", "h_ready", "trans", "trans_out", "pq_ready", "pq_out"))
    trans_out.by = 2
    pq_stored, h_stored, x_stored = Stage("pq_stored", 32), Stage("h_stored", 16), Stage("x_stored", 16)
    s_tot, s_totb, s_ready = sem("total"), sem("total_spread"), sem("next_layer_ready")
    s_fold, s_fold_out, s_deg = sem("folded"), sem("folded_out"), sem("degrees_moved")
    vector_steps, pool_steps = Count(sem("node_vector_steps")), Count(sem("node_pool_steps"))

    def pieces(width):
        return ((0, 0, 4 * width), (1, 4 * width, (CT - 4) * width))

    def node_phase(done, coming):
        hu = {0: HID, 1: HID, 2: D, 3: D}.get(done)
        hp = hid_of.get(coming)
        makes_pq = coming in (0, 2, 3)
        per_bank = 512 // (2 * hp) if makes_pq else 0
        pq_banks = (5, 6, 7, 4 if done is None else 0)[:-(-CT // per_bank)] if makes_pq else ()
        lag = 1 if done is not None else 0
        live = []
        if done in (0, 2, 3):
            live += [hidden] + [hidden_tanh] * (done == 3)
        if done == 1:
            live += [*tab_in, own, tab_sum, mix, mixT, mixT_out, h1, square1, var1, std1, h1n, h1T]
        if done is not None:
            live += [hidden_out, y_done, x_new]
        if coming is not None:
            live += [var, std, h_ready]
        if makes_pq:
            live += [trans, trans_out, pq_ready, pq_out, pq_stored]
        if coming == 1:
            live += [h_stored]
        if coming is None:
            live += [x_stored]

        def run(eng, stages, link=None):
            stages = [x for x in stages if x]
            far = max((b for b, _ in stages), default=0)
            lead = far + 1

            def step(i):
                for behind, stage in stages:
                    if not isinstance(i, int) or 0 <= i - behind < CHUNKS:
                        stage(i - behind)

            for i in range(lead):
                before = link.n if link else 0
                step(i)
            hold(eng)
            with eng.Fori(lead, CHUNKS) as i:
                if link:
                    link.enter(i, lead, link.n - before)
                step(i)
                hold(eng)
            if link:
                link.leave(CHUNKS - lead)
            for i in range(CHUNKS, CHUNKS + far):
                step(i)

        with nc.Block() as block:
            @block.tensor
            def _(pe):
                def transposes(src, width, banks, n):
                    hold(pe)
                    for k in range(CT):
                        mm = nc.tensor.transpose(bank[banks + k // 4][0:width, k % 4 * P:(k % 4 + 1) * P],
                                                 src[:, k * width:(k + 1) * width], ident[:, :])
                    mm.then_inc(n.sem, 1)

                def hidden_layer(i):
                    k = HID if done == 0 else D + 1
                    for b in range(2):
                        hidden_out.wait(pe, i, before=1, left=1 - b)
                        at = bass.ds(i * CN + b * HALF, HALF)
                        nc.tensor.matmul(bank[2 + b][0:hu, 0:HALF], w_u1h[done][:, 0:hu], hT[:, at],
                                         start=True, stop=False)
                        mm = nc.tensor.matmul(bank[2 + b][0:hu, 0:HALF], w_sum[done][0:k, 0:hu], acc[0:k, at],
                                              start=False, stop=True)
                        mm.then_inc(hidden.sem, 1)

                def mix_turned(i):
                    trans_out.wait(pe, i, before=2)
                    mixT_out.wait(pe, i, before=1)
                    mix.wait(pe, i)
                    transposes(mixed, D, 0, mixT)

                def h1_layer(i):
                    mixT_out.wait(pe, i)
                    hidden_out.wait(pe, i, before=1)
                    for k in range(CT):
                        mm = nc.tensor.matmul(bank[2 + k // 4][:, k % 4 * P:(k % 4 + 1) * P],
                                              mixTc[:, k * P:(k + 1) * P], w_u1h[1][0:D + 1, :],
                                              start=True, stop=True)
                    mm.then_inc(h1.sem, 1)

                def h1_turned(i):
                    h1n.wait(pe, i)
                    transposes(sq1, HID, 2, h1T)

                def output_layer(i):
                    hidden_out.wait(pe, i, left=1)
                    x_new.wait(pe, i, before=1)
                    for k in range(CT):
                        if k == 3:
                            hidden_out.wait(pe, i)
                        mm = nc.tensor.matmul(bank[4][:, k * D:(k + 1) * D], u1T[0:hu, k * P:(k + 1) * P],
                                              w_u2[done][0:hu, :], start=True, stop=True)
                    mm.then_inc(y_done.sem, 1)

                def h_turned(i):
                    trans_out.wait(pe, i, before=1)
                    if 0 in pq_banks:
                        pq_out.wait(pe, i, before=1)
                    if done == 1:
                        last = i + 1 if isinstance(i, int) and i + 1 < CHUNKS or not isinstance(i, int) else i
                        mixT_out.wait(pe, last)
                    h_ready.wait(pe, i)
                    transposes(xm, D, 0, trans)

                def first_layer(i):
                    trans_out.wait(pe, i, left=1)
                    pq_out.wait(pe, i, before=1)
                    for k in range(CT):
                        c = k % per_bank * 2 * hp
                        if c == 0 and pq_banks[k // per_bank] == 0:
                            trans_out.wait(pe, i)
                        mm = nc.tensor.matmul(bank[pq_banks[k // per_bank]][:, c:c + 2 * hp],
                                              hTc[:, k * P:(k + 1) * P], w_pq[coming][:, 0:2 * hp],
                                              start=True, stop=True)
                    mm.then_inc(pq_ready.sem, 1)

                if done == 3:
                    pe.wait_ge(s_tot, 1)
                    nc.tensor.matmul(bank[7][0:D + 1, 0:1], ones_r[D:D + 1, 0:D + 1], tot[D:D + 1, 0:1],
                                     start=True, stop=True).then_inc(s_totb, 1)
                    pe.wait_ge(s_tot, 3)
                if done == 0:
                    pe.wait_ge(s_deg, 16)
                if done == 1:
                    pe.wait_ge(s_mix1, 1)
                    run(pe, [(0, mix_turned), (0, h1_layer), (1, h_turned), (1, first_layer), (0, h1_turned),
                             (0, output_layer)])
                elif done == 3:
                    run(pe, [(1, output_layer), (0, hidden_layer)])
                elif done is not None:
                    run(pe, [(0, hidden_layer), makes_pq and (1, h_turned), (0, output_layer),
                             makes_pq and (1, first_layer)])
                else:
                    for l, k, h, at in FOLDED:
                        mm = nc.tensor.transpose(bank[2][0:D, at:at + k], w_agg[l][0:k, 0:D], ident[0:k, 0:k])
                    mm.then_inc(s_fold, 1)
                    pe.wait_ge(s_fold_out, 1)
                    for l, k, h, at in FOLDED:
                        nc.tensor.matmul(bank[3][0:k, at:at + h], aggT[:, at:at + k], w_u1a[l][:, 0:h],
                                         start=True, stop=True)
                        mm = nc.tensor.matmul(bank[3][0:1, HID + 2 * D + at:HID + 2 * D + at + h], b_agg[l][:, :],
                                              w_u1a[l][:, 0:h], start=True, stop=True)
                    mm.then_inc(s_fold, 1)
                    run(pe, [(0, h_turned), (0, first_layer)])

            @block.scalar
            def _(act):
                def copies(to, first, width, n=None):
                    for b, c, w in pieces(P):
                        a = nc.scalar.activation(to[0:width, c:c + w], bank[first + b][0:width, 0:w], ACT.Copy)
                    if n:
                        a.then_inc(n.sem, 1)

                def hidden_act(i):
                    y_done.wait(act, i, before=1)
                    for b in range(2):
                        hidden.wait(act, i, left=1 - b)
                        if done == 3:
                            a = nc.scalar.activation(xm[0:D, b * HALF:(b + 1) * HALF],
                                                     bank[2 + b][0:D, 0:HALF], ACT.Tanh, scale=0.5)
                        else:
                            a = nc.scalar.activation(u1T[0:hu, b * HALF:(b + 1) * HALF],
                                                     bank[2 + b][0:hu, 0:HALF], ACT.Relu)
                        a.then_inc((hidden_tanh if done == 3 else hidden_out).sem, 1)

                def own_part(i):
                    mix.wait(act, i, before=1)
                    nc.scalar.activation(own_h, h_all[:, bass.ds(i * CT * D, CT * D)], ACT.Copy,
                                         scale=eps1[:, 0:1]).then_inc(own.sem, 1)

                def mix_out(i):
                    mixT.wait(act, i)
                    h1.wait(act, i, before=1)
                    copies(mixTc, 0, D, mixT_out)

                def h1_square(i):
                    h1.wait(act, i)
                    h1T.wait(act, i, before=1)
                    for b, c, w in pieces(HID):
                        a = nc.scalar.activation(sq1[:, c:c + w], bank[2 + b][:, 0:w], ACT.Square)
                    a.then_inc(square1.sem, 1)

                def h1_deviation(i):
                    var1.wait(act, i)
                    nc.scalar.activation(st1[:, CT:2 * CT], st1[:, 0:CT], ACT.Sqrt, bias=eps_c[:, 0:1],
                                         scale=1.0 / HID).then_inc(std1.sem, 1)

                def h1_relu(i):
                    y_done.wait(act, i, before=1)
                    h1T.wait(act, i)
                    for b, c, w in pieces(P):
                        a = nc.scalar.activation(u1T[:, c:c + w], bank[2 + b][:, 0:w], ACT.Relu,
                                                 bias=ln_gb[:, 1:2], scale=ln_gb[:, 0:1])
                        a.then_inc(hidden_out.sem, 1)

                def deviation(i):
                    var.wait(act, i)
                    nc.scalar.activation(st[:, CT:2 * CT], st[:, 0:CT], ACT.Sqrt, bias=eps_c[:, 0:1],
                                         scale=1.0 / D).then_inc(std.sem, 1)

                def h_out(i):
                    pq_ready.wait(act, i, before=1)
                    trans.wait(act, i)
                    copies(hTc, 0, D, trans_out)
                    for b, c, w in pieces(P):
                        a = nc.scalar.activation(hT[0:D, bass.ds(i * CN + c, w)], bank[b][0:D, 0:w], ACT.Copy)
                    a.then_inc(trans_out.sem, 1)

                def tables_out(i):
                    pq_stored.wait(act, i, before=1)
                    pq_ready.wait(act, i)
                    step = per_bank * 2 * hp
                    for k, b in enumerate(pq_banks):
                        w = min(step, CT * 2 * hp - k * step)
                        a = nc.scalar.activation(pq[:, k * step:k * step + w], bank[b][:, 0:w], ACT.Copy)
                    a.then_inc(pq_out.sem, 1)

                if done is None:
                    act.wait_ge(s_fold, 1)
                    nc.scalar.activation(aggT, bank[2][0:D, 0:HID + D + D + 1], ACT.Copy).then_inc(s_fold_out, 1)
                    act.wait_ge(s_fold, 2)
                    nc.scalar.activation(b_sum[:, :], bank[3][0:1, HID + 2 * D:], ACT.Copy).then_inc(s_fold_out, 1)
                    for l, k, h, at in FOLDED:
                        nc.scalar.activation(w_sum[l][0:k, 0:h], bank[3][0:k, at:at + h], ACT.Copy)\
                            .then_inc(s_fold_out, 1)
                if done == 3:
                    run(act, [(0, hidden_act)])
                elif done == 1:
                    run(act, [(0, own_part), (0, mix_out), (1, deviation), (0, h1_square), (1, h_out),
                              (0, h1_deviation), (1, tables_out), (0, h1_relu)])
                else:
                    run(act, [coming is not None and (lag, deviation), done is None and (1, tables_out),
                              done is not None and (0, hidden_act),
                              makes_pq and (lag, h_out), done == 2 and (lag, tables_out)])

            @block.vector
            def _(dve):
                link = Link(dve, vector_steps)
                w = CT * D

                def hidden_silu(i):
                    y_done.wait(dve, i, before=1)
                    for b in range(2):
                        hidden_tanh.wait(dve, i, left=1 - b)
                        a = nc.vector.scalar_tensor_tensor(
                            u1T[0:D, b * HALF:(b + 1) * HALF], xm[0:D, b * HALF:(b + 1) * HALF], 1.0,
                            bank[2 + b][0:D, 0:HALF], ALU.add, ALU.mult)
                        a.then_inc(hidden_out.sem, 1)

                def h1_norm(i):
                    square1.wait(dve, i)
                    s3 = sq1.rearrange("p (c d) -> p c d", d=HID)
                    nc.vector.tensor_reduce(st1[:, 0:CT], s3, AX.X, ALU.add).then_inc(var1.sem, 1)
                    std1.wait(dve, i)
                    link(nc.vector.reciprocal(st1[:, 2 * CT:3 * CT], st1[:, CT:2 * CT]))
                    for b, c0, c1 in ((0, 0, 4), (1, 4, CT)):
                        a = nc.vector.tensor_tensor(
                            s3[:, c0:c1, :],
                            bank[2 + b][:, 0:(c1 - c0) * HID].rearrange("p (c d) -> p c d", d=HID),
                            st1[:, 2 * CT + c0:2 * CT + c1, None].to_broadcast((P, c1 - c0, HID)), ALU.mult)
                    a.then_inc(h1n.sem, 1)

                def x_update(i):
                    xc = x_all[:, bass.ds(i * w, w)]
                    y_done.wait(dve, i)
                    nc.vector.tensor_tensor(xc, xc, bank[4][:, 0:w], ALU.add).then_inc(x_new.sem, 1)

                def layernorm(i):
                    x3 = x_all[:, bass.ds(i * w, w)].rearrange("p (c d) -> p c d", d=D)
                    m3 = xm[:, 0:w].rearrange("p (c d) -> p c d", d=D)
                    q3 = sq[:, 0:w].rearrange("p (c d) -> p c d", d=D)
                    mean, inverse = st[:, 2 * CT:3 * CT], st[:, 3 * CT:4 * CT]
                    if done is not None:
                        x_new.wait(dve, i)
                    if makes_pq:
                        trans.wait(dve, i, before=1)
                    hold(dve)
                    link(nc.vector.tensor_reduce(mean, x3, AX.X, ALU.add))
                    link(nc.vector.tensor_scalar(mean, mean, 1.0 / D, None, ALU.mult))
                    link(nc.vector.tensor_tensor(m3, x3, mean[:, :, None].to_broadcast((P, CT, D)), ALU.subtract))
                    link(nc.vector.tensor_tensor(q3, m3, m3, ALU.mult))
                    nc.vector.tensor_reduce(st[:, 0:CT], q3, AX.X, ALU.add).then_inc(var.sem, 1)
                    std.wait(dve, i)
                    link(nc.vector.reciprocal(inverse, st[:, CT:2 * CT]))
                    link(nc.vector.tensor_tensor(m3, m3, inverse[:, :, None].to_broadcast((P, CT, D)), ALU.mult))
                    to = h_all[:, bass.ds(i * w, w)] if coming == 1 else xm[:, 0:w]
                    nc.vector.tensor_scalar(to, xm[:, 0:w], 0.0, None, ALU.max).then_inc(h_ready.sem, 1)
                    h_ready.wait(dve, i)

                if done == 3:
                    link(nc.vector.tensor_reduce(tot[D:D + 1, 0:1], acc[D:D + 1, 0:N_NODES], AX.X, ALU.add))
                    nc.vector.tensor_copy(tot[D:D + 1, 1:2], tot[D:D + 1, 0:1]).then_inc(s_tot, 1)
                    dve.wait_ge(s_totb, 1)
                    nc.vector.reciprocal(itot[:, :], bank[7][0:D + 1, 0:1]).then_inc(s_tot, 1)
                    dve.wait_ge(s_tot, 2)
                    nc.vector.tensor_scalar(w_sum[3][:, :], w_sum[3][:, :], itot[:, 0:1], None,
                                            ALU.mult).then_inc(s_tot, 1)
                if done == 1:
                    nc.vector.memset(mixTc[D:D + 1, :], 1.0).then_inc(s_mix1, 1)
                    run(dve, [(1, layernorm), (0, h1_norm), (0, x_update)], link)
                elif done == 3:
                    run(dve, [(1, x_update), (0, hidden_silu)], link)
                else:
                    run(dve, [(lag, layernorm), done is not None and (0, x_update)], link)
                if coming is not None:
                    x_all3 = x_all[:, :].rearrange("p (t d) -> p t d", d=D)
                    nc.vector.tensor_tensor(x_all3, x_all3, b_u2[coming][:, None, :].to_broadcast((P, TILES, D)),
                                            ALU.add).then_inc(s_ready, 1)
                if coming in (2, 3):
                    nc.vector.memset(acc[:, :], 0.0).then_inc(s_ready, 1)
                if coming == 3:
                    pq_stored.wait(dve, CHUNKS - 1)
                    for q in range(SLOTS):
                        nc.vector.memset(msg[q].rearrange("p (j h) -> p j h", h=HID + 1)[:, :, HID:HID + 1], 1.0)\
                            .then_inc(s_ready, 1)
                vector_steps.base += link.n

            @block.gpsimd
            def _(pool):
                link = Link(pool, pool_steps)
                w = CT * D

                def mixture(i):
                    tab_in[0].wait(pool, i)
                    link(nc.gpsimd.tensor_tensor(total, tabs[0], tabs[1], ALU.add))
                    for k in range(2, TABLES):
                        if k == TABLES // 2:
                            tab_in[1].wait(pool, i)
                        a = nc.gpsimd.tensor_tensor(total, total, tabs[k], ALU.add)
                        if k in (TABLES // 2 - 1, TABLES - 1):
                            a.then_inc(tab_sum.sem, 1)
                            tab_sum.wait(pool, i, left=int(k < TABLES - 1))
                        else:
                            link(a)
                    hold(pool)
                    link(nc.gpsimd.tensor_scalar(total, total, 0.0, None, ALU.max))
                    mixT.wait(pool, i, before=1)
                    own.wait(pool, i)
                    nc.gpsimd.tensor_tensor(mixed, total, own_h, ALU.add).then_inc(mix.sem, 1)
                    mix.wait(pool, i)

                if done == 1:
                    run(pool, [(0, mixture)], link)
                    pool_steps.base += link.n

            @block.sync
            def _(sp):
                def tables_in(i):
                    for k in range(TABLES):
                        if k % (TABLES // 2) == 0:
                            tab_sum.wait(sp, i, before=1, left=int(k == 0))
                        sp.dma_start(tabs[k].rearrange("p (c d) -> p c d", d=D),
                                     sums[k][0:NPAD, :].rearrange("(t p) d -> p t d", p=P)[:, bass.ds(i * CT, CT), :])\
                            .then_inc(tab_in[k // (TABLES // 2)].sem, 16)

                def store_tables(i):
                    pq_out.wait(sp, i)
                    v = pq[:, 0:CT * 2 * hp].rearrange("p (c h) -> p c h", h=2 * hp)
                    for tab, c in ((p_tab[coming], 0), (q_tab[coming], hp)):
                        sp.dma_start(tab.rearrange("(t p) h -> p t h", p=P)[:, bass.ds(i * CT, CT), :],
                                     v[:, :, c:c + hp]).then_inc(pq_stored.sem, 16)

                def store_h(i):
                    h_ready.wait(sp, i)
                    sp.dma_start(h_tab.rearrange("(t p) d -> p t d", p=P)[:, bass.ds(i * CT, CT), :],
                                 h_all[:, bass.ds(i * CT * D, CT * D)].rearrange("p (c d) -> p c d", d=D))\
                        .then_inc(h_stored.sem, 16)

                def store_x(i):
                    x_new.wait(sp, i)
                    full = CT if not isinstance(i, int) or i < CHUNKS - 1 else whole - (CHUNKS - 1) * CT
                    xv = x_all[:, bass.ds(i * CT * D, full * D)].rearrange("p (c d) -> p c d", d=D)
                    sp.dma_start(out[0:whole * P, :].rearrange("(t p) d -> p t d", p=P)[:, bass.ds(i * CT, full), :],
                                 xv).then_inc(x_stored.sem, 16)

                if coming == 3:
                    for q in range(SLOTS):
                        for o, w1 in ((0, "L3_gnn_Wa1"), (D, "L3_gnn_W1")):
                            sp.dma_start(rows[q][WIN:WIN + D_EDGE, o:o + D], t[w1][2 * D:2 * D + D_EDGE, :])\
                                .then_inc(s_w3, 16)
                if done == 0:
                    sp.dma_start(hT[D + 1:D + 2, :], deg).then_inc(s_deg, 16)
                if done == 1:
                    run(sp, [(0, tables_in), (2, store_tables)])
                elif done is None:
                    for i in range(CHUNKS):
                        store_tables(i)
                        for k in range(i * TABLES // CHUNKS, (i + 1) * TABLES // CHUNKS):
                            sp.dma_start(sums[k].rearrange("(p a r) d -> p a (r d)", p=P, a=5),
                                         zero_row[:, None, :].to_broadcast((P, 5, SUM_ROW))).then_inc(s_zt, 16)
                elif makes_pq:
                    run(sp, [(0, store_tables)])
                elif coming == 1:
                    run(sp, [(0, store_h)])
                else:
                    for i in range(CHUNKS):
                        store_x(i)
                    sp.dma_start(out[whole * P:N_NODES, :], x_all[0:rest, whole * D:TILES * D])\
                        .then_inc(s_out, 16)
                    x_stored.wait(sp, CHUNKS - 1)
                    sp.wait_ge(s_out, 16)
                if makes_pq:
                    pq_stored.wait(sp, CHUNKS - 1)
                if coming == 1:
                    h_stored.wait(sp, CHUNKS - 1)
                if coming == 3:
                    sp.wait_ge(s_w3, 16 * 2 * SLOTS)
                if done is None:
                    sp.wait_ge(s_zt, 16 * TABLES)
                    sp.wait_ge(s_fold_out, 2)
                    for l, k, h, at in FOLDED[:2]:
                        sp.dma_start(w_u1h[l][D + 1:D + 2, 0:h], b_sum[:, at:at + h]).then_inc(s_fb, 16)
                    sp.wait_ge(s_fb, 32)
        for s in live:
            s.end()

    s_fb, s_mix1, s_merged = sem("folded_bias_in"), sem("row_of_ones"), sem("groups_merged")
    s_out, s_w3, s_held = sem("result_stored"), sem("weights3_in"), sem("waits_held")

    def counts(kind, names):
        return {n: Count(sem(f"{kind}_{n}")) for n in names}

    NAMES = (*(f"{n}{q}" for n in ("rows_moved", "idx_in", "win_in") for q in range(SLOTS)),
             "pick_ready", "sum_ready", "pre_ready", "z_ready", "msg_ready", "seg_ready", "acc_done", "deg_done",
             "tanh_ready", "max_ready", "maxT_ready", "max1_ready", "max_biased", "max_kept",
             "maxb_ready", "nmax_ready", "prob_ready", "comb_ready", "comb_out", "equal_ready", "index_ready",
             "masked", "merge", "acc2_zeroed",
             "vector_steps")
    in_order, windowed = counts("o", NAMES), counts("w", NAMES)

    def edge_pass(layer, c, window):
        hid = {0: HID, 1: D, 2: D, 3: HID}[layer]
        feat = layer in (0, 3)
        depth = WIN + (D_EDGE if feat else 0)
        loads = 3 if feat or layer == 1 else 2
        loads += layer == 1
        softmax = layer == 3
        table_q = h_tab if layer == 1 else q_tab[layer]
        per = dict.fromkeys(NAMES, GROUPS)
        for q in range(SLOTS):
            per[f"idx_in{q}"], per[f"win_in{q}"] = 16 * ITERS, 16 * loads * ITERS
            per[f"rows_moved{q}"] = 16 * SUB * ITERS
        per["vector_steps"] = {0: 0, 1: 4 * GROUPS, 2: 0, 3: 2 * GROUPS + 3}[layer]
        per["merge"], per["acc2_zeroed"] = 3, 1
        live = {f"{n}{q}" for n in ("idx_in", "win_in", "rows_moved") for q in range(SLOTS)}
        live |= {"pick_ready", "pre_ready", "z_ready", "msg_ready", "vector_steps"}
        if layer == 1:
            live |= {"comb_ready", "comb_out", "equal_ready", "index_ready"}
            if window is not None:
                live |= {"masked"}
                per["vector_steps"] += 3 * GROUPS
        else:
            live |= {"sum_ready", "seg_ready", "acc_done"}
        if layer == 0:
            live |= {"deg_done"}
        if softmax:
            beyond = GROUPS - N_EDGES // GE
            per["vector_steps"] += 4 * beyond if window is None else 6 * GROUPS + 2 * beyond + 2
            live |= {"tanh_ready", "max_ready", "maxT_ready", "max1_ready", "max_biased", "max_kept",
                     "maxb_ready", "nmax_ready", "prob_ready", "merge", "acc2_zeroed"}
        for n, count in c.items():
            count.begin(per[n] if n in live else 0, window)
            if window is not None and n.startswith("rows_moved"):
                count.begin(0, None)

        def run(eng, stages, link=None):
            last = -(-max(b for b, _ in stages) // SLOTS)

            def iteration(i):
                for r in range(SLOTS):
                    for behind, stage in stages:
                        q, ii = (r - behind) % SLOTS, i + (r - behind) // SLOTS
                        if not isinstance(i, int) or 0 <= ii < ITERS:
                            stage(q, ii)

            lead = LEAD if last else 1
            for i in range(lead):
                before = link.n if link else 0
                iteration(i)
            with eng.Fori(lead, ITERS) as i:
                if link:
                    link.enter(i, lead, link.n - before)
                iteration(i)
            if link:
                link.leave(ITERS - lead)
            for i in range(ITERS, ITERS + last):
                iteration(i)

        def g(q, i):
            return i * SLOTS + q + 1

        def sub(tile, j, width):
            return tile[:, j * width:(j + 1) * width]

        def as3(tile, width, stride=None):
            return tile[:, 0:SUB * (stride or width)].rearrange("p (j h) -> p j h", h=stride or width)[:, :, 0:width]

        def z3(q):
            return as3(z[q], hid)

        def m3(q, a=0, b=hid):
            return msg[q][:, :].rearrange("p (j h) -> p j h", h=HID + 1)[:, :, a:b]

        with nc.Block() as block:
            @block.sync
            def _(sp):
                def load(q, i):
                    n = i * SLOTS + q
                    if layer == 1:
                        c["index_ready"].wait(sp, g(q, i) - SLOTS)
                    else:
                        c[f"rows_moved{q}"].wait(sp, 16 * SUB * i)
                    sp.dma_start(idx[q][:, :], t["src_tiles"][:, bass.ds(n, 1), :].rearrange("p g j -> p (g j)"))\
                        .then_inc(c[f"idx_in{q}"].sem, 16)
                    base = sp.value_load(base_row[0:1, bass.ds(n, 1)], min_val=0, max_val=NPAD - WIN)
                    c["pre_ready"].wait(sp, g(q, i) - SLOTS)
                    s = c[f"win_in{q}"].sem
                    sp.dma_start(dst_b[q], dst_f[bass.ds(n, 1), :].to_broadcast((WIN, GE)))\
                        .then_inc(s, 16)
                    sp.dma_start(rows[q][0:WIN, 0:hid], table_q[bass.ds(base, WIN), :]).then_inc(s, 16)
                    if feat:
                        sp.dma_start(stack[q][WIN:depth, :],
                                     t["feat_cols"][bass.ds(n, 1), :, :].rearrange("g k e -> (g k) e"))\
                            .then_inc(s, 16)
                    if layer == 1:
                        c["msg_ready"].wait(sp, g(q, i) - SLOTS)
                        c["equal_ready"].wait(sp, g(q, i) - SLOTS)
                        sp.dma_start(z[q][:, 0:SUB * D],
                                     t["edge64"][bass.ds(n, 1), :, :].rearrange("g p e -> (g p) e"))\
                            .then_inc(s, 16)
                        sp.dma_start(src_b[q], t["src_cols"][bass.ds(n, 1), :].to_broadcast((P, GE)))\
                            .then_inc(s, 16)

                run(sp, [(0, load)])

            @block.gpsimd
            def _(pool):
                def gather(q, i):
                    c[f"idx_in{q}"].wait(pool, 16 * (i + 1))
                    c["msg_ready"].wait(pool, g(q, i) - SLOTS)
                    hold(pool)
                    for j in range(SUB):
                        pool.indirect_dma_start(
                            z[q][:, j * hid:(j + 1) * hid], None, p_tab[layer],
                            bass.IndirectOffsetOnAxis(ap=idx[q][:, j:j + 1], axis=0))\
                            .then_inc(c[f"rows_moved{q}"].sem, 16)

                def scatter(q, i):
                    c["index_ready"].wait(pool, g(q, i))
                    c["comb_out"].wait(pool, g(q, i))
                    before = (q - 2) % SLOTS
                    c[f"rows_moved{before}"].wait(pool, 16 * SUB * (i + (q >= 2)))
                    hold(pool)
                    for j in range(SUB):
                        pool.indirect_dma_start(
                            sums[q % 2 * SUB + j],
                            bass.IndirectOffsetOnAxis(ap=idx_e[q][:, j:j + 1], axis=0),
                            comb[q][:, j * D:(j + 1) * D], None, compute_op=ALU.add)\
                            .then_inc(c[f"rows_moved{q}"].sem, 16)

                run(pool, [(0, scatter if layer == 1 else gather)])
                if softmax:
                    c["msg_ready"].wait(pool, GROUPS)
                    c["max_ready"].wait(pool, GROUPS)
                    hold(pool)
                    nc.gpsimd.memset(acc2, 0.0).then_inc(c["acc2_zeroed"].sem, 1)
                for q in range(SLOTS):
                    c[f"rows_moved{q}"].wait(pool, 16 * SUB * ITERS)

            @block.tensor
            def _(pe):
                def pre(q, i):
                    c["pick_ready"].wait(pe, g(q, i))
                    c[f"win_in{q}"].wait(pe, 16 * loads * (i + 1))
                    c["z_ready"].wait(pe, g(q, i) - 2)
                    for j in range(SUB):
                        mm = nc.tensor.matmul(bank[q % 2][:, j * hid:(j + 1) * hid],
                                              stack[q][0:depth, j * P:(j + 1) * P], rows[q][0:depth, 0:hid],
                                              start=True, stop=True)
                    mm.then_inc(c["pre_ready"].sem, 1)

                def seg(q, i):
                    c["sum_ready"].wait(pe, g(q, i))
                    c["msg_ready"].wait(pe, g(q, i))
                    c["acc_done"].wait(pe, g(q, i) - 2)
                    if layer == 0:
                        c["deg_done"].wait(pe, g(q, i) - 2)
                    lo, hi = (D, HID + 1) if softmax else (0, hid)
                    for j in range(SUB):
                        mm = nc.tensor.matmul(bank[2 + q % 2][0:hi - lo, 0:WIN],
                                              msg[q][:, j * (HID + 1) + lo:j * (HID + 1) + hi],
                                              sub(onehot[q], j, WIN), start=j == 0, stop=j == SUB - 1)
                    if layer == 0:
                        for j in range(SUB):
                            mm = nc.tensor.matmul(bank[4 + q % 2][0:1, 0:WIN], ones_c[:, :],
                                                  sub(onehot[q], j, WIN), start=j == 0, stop=j == SUB - 1)
                    mm.then_inc(c["seg_ready"].sem, 1)

                def max_across(q, i):
                    c["max_ready"].wait(pe, g(q, i))
                    c["max1_ready"].wait(pe, g(q, i) - 2)
                    nc.tensor.transpose(bank[4 + q % 2][0:1, 0:P], gmax[q % 2][:, :], ident[:, :])\
                        .then_inc(c["maxT_ready"].sem, 1)

                def max_spread(q, i):
                    c["max_biased"].wait(pe, g(q, i))
                    c["nmax_ready"].wait(pe, g(q, i) - 2)
                    nc.tensor.matmul(bank[6 + q % 2][:, 0:1], ones_r[0:1, :], biased[q % 2][:, :],
                                     start=True, stop=True).then_inc(c["maxb_ready"].sem, 1)

                def combine(q, i):
                    c["equal_ready"].wait(pe, g(q, i))
                    c["msg_ready" if window is None else "masked"].wait(pe, g(q, i))
                    c["comb_out"].wait(pe, g(q, i) - 2)
                    for j in range(SUB):
                        mm = nc.tensor.matmul(bank[2 + q % 2][:, j * D:(j + 1) * D], sub(equal[q % 2], j, P),
                                              m3(q)[:, j, :], start=True, stop=True)
                    mm.then_inc(c["comb_ready"].sem, 1)

                if layer == 1:
                    run(pe, [(0, pre), (2, combine)])
                elif softmax:
                    run(pe, [(5, seg), (3, max_spread), (2, max_across), (0, pre)])
                    c["merge"].wait(pe, 2)
                    nc.tensor.matmul(bank[7][0:D + 1, 0:GROUPS + 1], ones_r[0:1, 0:D + 1], scale_row[:, :],
                                     start=True, stop=True).then_inc(c["merge"].sem, 1)
                else:
                    run(pe, [(0, pre), (2, seg)])

            @block.scalar
            def _(act):
                def relu(q, i):
                    c["z_ready"].wait(act, g(q, i))
                    if layer == 1:
                        c["comb_ready"].wait(act, g(q, i) - SLOTS)
                    else:
                        c["seg_ready"].wait(act, g(q, i) - SLOTS)
                    nc.scalar.activation(m3(q), z3(q), ACT.Relu).then_inc(c["msg_ready"].sem, 1)

                def tanh(q, i):
                    c["z_ready"].wait(act, g(q, i))
                    c["msg_ready"].wait(act, g(q, i) - 2)
                    nc.scalar.activation(half[q % 2][:, :], z[q][:, :], ACT.Tanh, scale=0.5)\
                        .then_inc(c["tanh_ready"].sem, 1)

                def bias_max(q, i):
                    c["max1_ready"].wait(act, g(q, i))
                    c["maxb_ready"].wait(act, g(q, i) - 2)
                    nc.scalar.activation(biased[q % 2][:, :], gmax1[q % 2][:, :], ACT.Identity,
                                         bias=ba2[0:1, 0:1]).then_inc(c["max_biased"].sem, 1)

                def exp(q, i):
                    c["max_biased"].wait(act, g(q, i))
                    nc.scalar.activation(gmax_row[:, bass.ds(i * SLOTS + q, 1)], biased[q % 2][:, :],
                                         ACT.Copy).then_inc(c["max_kept"].sem, 1)
                    c["maxb_ready"].wait(act, g(q, i))
                    nc.scalar.activation(nmax[q % 2][:, :], bank[6 + q % 2][:, 0:1], ACT.Identity, scale=-1.0,
                                         bias=ba2[:, 0:1]).then_inc(c["nmax_ready"].sem, 1)
                    c["nmax_ready"].wait(act, g(q, i))
                    c["sum_ready"].wait(act, g(q, i) - 2)
                    nc.scalar.activation(prob[q % 2][:, :], logit[q % 2][:, :], ACT.Exp, bias=nmax[q % 2][:, 0:1])\
                        .then_inc(c["prob_ready"].sem, 1)

                def keep(q, i):
                    c["seg_ready"].wait(act, g(q, i))
                    nc.scalar.activation(parts[:, bass.ds((i * SLOTS + q) * WIN, WIN)],
                                         bank[2 + q % 2][0:D + 1, 0:WIN], ACT.Copy).then_inc(c["acc_done"].sem, 1)

                def combined(q, i):
                    c["comb_ready"].wait(act, g(q, i))
                    c[f"rows_moved{q}"].wait(act, 16 * SUB * i)
                    nc.scalar.activation(comb[q], bank[2 + q % 2][:, 0:SUB * D], ACT.Copy)\
                        .then_inc(c["comb_out"].sem, 1)

                if layer == 1:
                    run(act, [(1, relu), (2, combined)])
                elif softmax:
                    run(act, [(6, keep), (4, exp), (3, bias_max), (1, tanh)])
                    c["merge"].wait(act, 1)
                    nc.scalar.activation(scale_row[:, :], gmax_row[:, :], ACT.Exp, bias=gm1[:, 1:2])\
                        .then_inc(c["merge"].sem, 1)
                else:
                    run(act, [(1, relu)])

            @block.vector
            def _(dve):
                link = Link(dve, c["vector_steps"])

                def pick(q, i):
                    c[f"win_in{q}"].wait(dve, 16 * loads * (i + 1))
                    nc.vector.tensor_scalar(stack[q][0:WIN, :], dst_b[q],
                                            base_col[:, bass.ds(i * SLOTS + q, 1)], None,
                                            ALU.is_equal).then_inc(c["pick_ready"].sem, 1)

                def window_onehot(q, i):
                    c["seg_ready"].wait(dve, g(q, i) - SLOTS)
                    return nc.vector.tensor_tensor(
                        onehot[q][:, :].rearrange("p (j w) -> p j w", w=WIN),
                        dst_rel[:, bass.ds((i * SLOTS + q) * SUB, SUB)][:, :, None].to_broadcast((P, SUB, WIN)),
                        iota_w[:, None, :].to_broadcast((P, SUB, WIN)), ALU.is_equal)

                def plain_onehot(q, i):
                    window_onehot(q, i).then_inc(c["sum_ready"].sem, 1)

                def add(q, i):
                    c["pre_ready"].wait(dve, g(q, i))
                    if layer != 1:
                        c[f"rows_moved{q}"].wait(dve, 16 * SUB * (i + 1))
                    nc.vector.tensor_tensor(z[q][:, 0:SUB * hid], z[q][:, 0:SUB * hid],
                                            bank[q % 2][:, 0:SUB * hid], ALU.add).then_inc(c["z_ready"].sem, 1)

                def accumulate(q, i):
                    hold(dve)
                    base = dve.value_load(base_row[0:1, bass.ds(i * SLOTS + q, 1)], min_val=0, max_val=NPAD - WIN)
                    at = bass.ds(base, WIN)
                    c["seg_ready"].wait(dve, g(q, i))
                    c["acc_done"].wait(dve, g(q, i) - 1)
                    nc.vector.tensor_tensor(acc[0:hid, at], acc[0:hid, at], bank[2 + q % 2][0:hid, 0:WIN],
                                            ALU.add).then_inc(c["acc_done"].sem, 1)
                    if layer == 0:
                        c["deg_done"].wait(dve, g(q, i) - 1)
                        nc.vector.tensor_tensor(deg[:, at], deg[:, at], bank[4 + q % 2][0:1, 0:WIN],
                                                ALU.add).then_inc(c["deg_done"].sem, 1)

                def silu(q, i):
                    c["tanh_ready"].wait(dve, g(q, i))
                    c["seg_ready"].wait(dve, g(q, i) - SLOTS)
                    nc.vector.scalar_tensor_tensor(m3(q), half[q % 2][:, :].rearrange("p (j h) -> p j h", h=HID), 1.0,
                                                   z3(q), ALU.add, ALU.mult).then_inc(c["msg_ready"].sem, 1)
                    c["msg_ready"].wait(dve, g(q, i))
                    p3 = prod[:, 0:SUB * D].rearrange("p (j h) -> p j h", h=D)
                    link(nc.vector.tensor_tensor(p3, m3(q, 0, D), wa2[:, None, :].to_broadcast((P, SUB, D)),
                                                 ALU.mult))
                    c["prob_ready"].wait(dve, g(q, i) - 2)
                    link(nc.vector.tensor_reduce(logit[q % 2][:, :], p3, AX.X, ALU.add))
                    drop_logits(q, i)
                    c["maxT_ready"].wait(dve, g(q, i) - 2)
                    nc.vector.tensor_reduce(gmax[q % 2][:, :], logit[q % 2][:, :], AX.X,
                                            ALU.max).then_inc(c["max_ready"].sem, 1)

                def drop_logits(q, i):
                    at = bass.ds((i * SLOTS + q) * SUB, SUB)
                    among, low = dup[:, 2 * SUB:3 * SUB], dup[:, 3 * SUB:4 * SUB]
                    beyond = isinstance(i, int) and i * SLOTS + q >= N_EDGES // GE
                    if window is not None:
                        link(nc.vector.tensor_scalar(among, dst_rel[:, at], 0.0, None, ALU.is_ge))
                        link(nc.vector.tensor_scalar(low, dst_rel[:, at], float(WIN), None, ALU.is_lt))
                        link(nc.vector.tensor_tensor(among, among, low, ALU.mult))
                    if beyond:
                        link(nc.vector.tensor_scalar(low if window is not None else among, dst_i[:, at],
                                                     float(N_NODES), None, ALU.is_lt))
                        if window is not None:
                            link(nc.vector.tensor_tensor(among, among, low, ALU.mult))
                    if window is not None or beyond:
                        link(nc.vector.tensor_scalar(low, among, -1.0, FAR, ALU.add, ALU.mult))
                        link(nc.vector.tensor_tensor(logit[q % 2][:, :], logit[q % 2][:, :], among, ALU.mult))
                        link(nc.vector.tensor_tensor(logit[q % 2][:, :], logit[q % 2][:, :], low, ALU.add))

                def group_max(q, i):
                    c["maxT_ready"].wait(dve, g(q, i))
                    c["max_biased"].wait(dve, g(q, i) - 2)
                    nc.vector.tensor_reduce(gmax1[q % 2][:, :], bank[4 + q % 2][0:1, 0:P], AX.X,
                                            ALU.max).then_inc(c["max1_ready"].sem, 1)

                def weigh(q, i):
                    c["prob_ready"].wait(dve, g(q, i))
                    c["seg_ready"].wait(dve, g(q, i) - SLOTS)
                    for j in range(SUB):
                        a = nc.vector.tensor_scalar(
                            sub(onehot[q], j, WIN), iota_w[:, :],
                            dst_rel[:, bass.ds((i * SLOTS + q) * SUB + j, 1)], prob[q % 2][:, j:j + 1],
                            ALU.is_equal, ALU.mult)
                    a.then_inc(c["sum_ready"].sem, 1)

                def same(q, i):
                    c[f"idx_in{q}"].wait(dve, 16 * (i + 1))
                    c["comb_ready"].wait(dve, g(q, i) - 2)
                    e3 = equal[q % 2].rearrange("p (j e) -> p j e", e=P)
                    d3 = prod[:, :].rearrange("p (j e) -> p j e", e=P)
                    nc.vector.tensor_tensor(e3, src_b[q].rearrange("p (j e) -> p j e", e=P),
                                            idx[q][:, :, None].to_broadcast((P, SUB, P)),
                                            ALU.is_equal).then_inc(c["equal_ready"].sem, 1)
                    c["equal_ready"].wait(dve, g(q, i))
                    link(nc.vector.tensor_tensor(d3, e3, earlier[:, None, :].to_broadcast((P, SUB, P)), ALU.mult))
                    link(nc.vector.tensor_reduce(dup[:, 0:SUB], d3, AX.X, ALU.max))
                    link(nc.vector.tensor_scalar(dup[:, SUB:2 * SUB], idx[q][:, :], dummy[:, 0:1], None,
                                                 ALU.subtract))
                    link(nc.vector.tensor_tensor(dup[:, SUB:2 * SUB], dup[:, SUB:2 * SUB], dup[:, 0:SUB], ALU.mult))
                    c[f"rows_moved{q}"].wait(dve, 16 * SUB * i)
                    nc.vector.tensor_tensor(idx_e[q][:, :], idx[q][:, :], dup[:, SUB:2 * SUB],
                                            ALU.subtract).then_inc(c["index_ready"].sem, 1)

                def mask(q, i):
                    rel = dst_rel[:, bass.ds((i * SLOTS + q) * SUB, SUB)]
                    link(nc.vector.tensor_scalar(dup[:, 2 * SUB:3 * SUB], rel, 0.0, None, ALU.is_ge))
                    link(nc.vector.tensor_scalar(dup[:, 3 * SUB:4 * SUB], rel, float(WIN), None, ALU.is_lt))
                    link(nc.vector.tensor_tensor(dup[:, 2 * SUB:3 * SUB], dup[:, 2 * SUB:3 * SUB],
                                                 dup[:, 3 * SUB:4 * SUB], ALU.mult))
                    c["msg_ready"].wait(dve, g(q, i))
                    nc.vector.tensor_tensor(m3(q), m3(q),
                                            dup[:, 2 * SUB:3 * SUB][:, :, None].to_broadcast((P, SUB, D)),
                                            ALU.mult).then_inc(c["masked"].sem, 1)

                if layer == 1:
                    run(dve, [(0, pick), (1, add), (1, same)] + [(1, mask)] * (window is not None), link)
                elif softmax:
                    run(dve, [(5, weigh), (3, group_max), (2, silu), (1, add), (0, pick)], link)
                    c["max_kept"].wait(dve, GROUPS)
                    link(nc.vector.tensor_reduce(gm1[:, 0:1], gmax_row[:, :], AX.X, ALU.max))
                    nc.vector.tensor_scalar(gm1[:, 1:2], gm1[:, 0:1], -1.0, None, ALU.mult)\
                        .then_inc(c["merge"].sem, 1)
                    c["merge"].wait(dve, 3)
                    c["acc2_zeroed"].wait(dve, 1)
                    c["acc_done"].wait(dve, GROUPS)
                    if window is not None:
                        link(nc.vector.tensor_scalar(acc[0:D + 1, :], acc[0:D + 1, :],
                                                     bank[7][0:D + 1, GROUPS:GROUPS + 1], None, ALU.mult))
                        link(nc.vector.tensor_copy(gmax_row[:, GROUPS:], gm1[:, 0:1]))
                    v = parts[:, :].rearrange("p (g w) -> p g w", w=WIN)
                    link(nc.vector.tensor_tensor(
                        v, v, bank[7][0:D + 1, 0:GROUPS][:, :, None].to_broadcast((D + 1, GROUPS, WIN)), ALU.mult))

                    hold(dve)
                    with dve.Fori(0, GROUPS // MERGED) as i:
                        dve.sem_clear(s_merged)
                        _, bases = nc.values_load_multi_w_load_instructions(
                            base_row[0:1, bass.ds(i * MERGED, MERGED)], engines=(mybir.EngineType.DVE,),
                            min_val=0, max_val=NPAD - WIN, skip_runtime_bounds_check_because="made with a minimum")
                        for k, base in enumerate(bases):
                            to = (acc, acc2)[k % 2][0:D + 1, bass.ds(base, WIN)]
                            if k > 1:
                                dve.wait_ge(s_merged, k - 1)
                            nc.vector.tensor_tensor(to, to, parts[:, bass.ds((i * MERGED + k) * WIN, WIN)],
                                                    ALU.add).then_inc(s_merged, 1)
                        dve.wait_ge(s_merged, MERGED)
                        hold(dve)
                    link(nc.vector.tensor_tensor(acc[0:D + 1, :], acc[0:D + 1, :], acc2, ALU.add))
                    hold(dve)
                else:
                    run(dve, [(0, pick), (0, plain_onehot), (1, add), (3, accumulate)], link)
                assert link.n == per["vector_steps"], (layer, link.n, per["vector_steps"])
        for count in c.values():
            count.end(1 if window is None else WINDOWS)
        if window is not None:
            with nc.Block() as block:
                @block.gpsimd
                def _(pool):
                    pool.inc_swdge_sem([c[f"rows_moved{q}"].sem for q in range(SLOTS)],
                                       [16 * SUB * ITERS] * SLOTS, mode="sub")

    def next_window():
        with nc.Block() as block:
            @block.vector
            def _(dve):
                n = [0]

                def link(ins):
                    n[0] += 1
                    ins.then_inc(s_next, 1)
                    dve.wait_ge(s_next, n[0])

                dve.sem_clear(s_next)
                link(nc.vector.tensor_scalar(win_id[:, :], win_id[:, :], float(WIN), None, ALU.add))
                link(nc.vector.tensor_tensor(dup[:, 0:1], win_id[:, :], place[:, :], ALU.add))
                nc.vector.tensor_copy(base_row[:, :], win_id[0:1, 0:1].to_broadcast((1, GROUPS)))
                nc.vector.tensor_copy(base_col, dup[DST_AT:DST_AT + WIN, 0:1].to_broadcast((WIN, GROUPS)))
                link(nc.vector.tensor_scalar(dst_rel[:, :], dst_i[:, :], win_id[:, 0:1], None, ALU.subtract))

    def first_window():
        with nc.Block() as block:
            @block.vector
            def _(dve):
                nc.vector.memset(win_id[:, :], -float(WIN))

    s_next = sem("next_window")

    def edge_phase(layer):
        with nc.If(widest < WIN):
            edge_pass(layer, in_order, None)
        with nc.Else():
            first_window()
            with nc.Fori(0, WINDOWS) as w:
                next_window()
                edge_pass(layer, windowed, w)

    node_phase(None, 0)
    for layer in range(4):
        edge_phase(layer)
        node_phase(layer, layer + 1 if layer < 3 else None)


def kernel(**inputs):
    import numpy as np
    import concourse.bacc as bacc
    from concourse.bass_utils import run_bass_kernel_spmd

    nc = bacc.Bacc("TRN2", target_bir_lowering=False, num_devices=1)
    a = {k: np.ascontiguousarray(v) for k, v in inputs.items()}

    def padded(v, fill):
        out = np.full((GROUPS * GE, *v.shape[1:]), fill, v.dtype)
        out[:N_EDGES] = v
        return out

    src, dst = (padded(a.pop(k), N_NODES) for k in ("src", "dst"))
    feat = padded(a.pop("edge_attr_32"), 0).reshape(GROUPS, P, SUB, D_EDGE)
    a["edge64"] = padded(a.pop("edge_attr_64"), 0).reshape(GROUPS, P, SUB * D)
    a["feat_cols"] = np.ascontiguousarray(feat.transpose(0, 3, 2, 1)).reshape(GROUPS, D_EDGE, GE)
    a["dst_groups"] = dst.reshape(GROUPS, GE)
    for name, v in (("src", src), ("dst", dst)):
        v = v.reshape(GROUPS, P, SUB)
        a[name + "_tiles"] = np.ascontiguousarray(v.transpose(1, 0, 2))
        a[name + "_cols"] = np.ascontiguousarray(v.transpose(0, 2, 1)).reshape(GROUPS, GE)
    t = {k: nc.dram_tensor("in_" + k, v.shape, mybir.dt.from_np(v.dtype), kind="ExternalInput").ap()
         for k, v in a.items()}
    out = nc.dram_tensor("out", (N_NODES, D), F32, kind="ExternalOutput").ap()
    gnn(nc, t, out)
    r = run_bass_kernel_spmd(nc, [{"in_" + k: v for k, v in a.items()}], core_ids=[0])
    return r.results[0]["out"]
```
